# Optimizing a Trainium2 kernel written in Bass

```python
import numpy as np
import jax
import jax.numpy as jnp

def _softmax(x, axis=-1):
    return jax.nn.softmax(x, axis=axis)

def _gelu(x):
    return jax.nn.gelu(x, approximate=True)

def _silu(x):
    return jax.nn.silu(x)

def _sigmoid(x):
    return jax.nn.sigmoid(x)

def _layernorm(x, axis=-1, eps=1e-05):
    m = jnp.mean(x, axis=axis, keepdims=True)
    v = jnp.var(x, axis=axis, keepdims=True)
    return (x - m) / jnp.sqrt(v + eps)

def _scatter_add(tgt, idx, src, axis=0):
    return tgt.at[idx].add(src)

def _segment_sum(src, seg, n):
    return jax.ops.segment_sum(src, seg, n)
kernel_name = 'mk_flamingo_gated_d1_seqx_r4_c9df8a'

def setup_inputs(seed: int=0):
    np.random.seed(seed)
    _w = jnp.asarray

    def _rec_inputs():
        import jax
        import jax.numpy as jnp
        _rk = jax.random.key(seed)
        x = 7.22e-05 + 1 * jax.random.normal(jax.random.fold_in(_rk, 1), (16, 128, 1024), jnp.float32)
        _lenS = 128 - jax.random.randint(jax.random.fold_in(_rk, 7), (16,), 0, max(1, 128 // 4) + 1, jnp.int32)
        _lenS2 = 128 - jax.random.randint(jax.random.fold_in(_rk, 8), (16,), 0, max(1, 128 // 4) + 1, jnp.int32)
        _ctx_4096P = jax.random.normal(jax.random.fold_in(_rk, 11), (16, 16, 1024), jnp.float32)
        _ctx_4096c = jax.random.dirichlet(jax.random.fold_in(_rk, 511), 0.3 * jnp.ones((16,), jnp.float32), (16, 128))
        _ctx_4096t = jnp.einsum('bsk,bkd->bsd', _ctx_4096c, _ctx_4096P)
        _ctx_4096t = _ctx_4096t * jax.lax.rsqrt(jnp.mean(jnp.square(_ctx_4096t)) + 1e-12) * 0.953939
        ctx_4096 = 4.13588e-05 + 0.999923 * (_ctx_4096t + 0.3 * jax.random.normal(jax.random.fold_in(_rk, 611), (16, 128, 1024), jnp.float32))
        _g = jax.random.normal(jax.random.fold_in(_rk, 9001), (2, 1), jnp.float32)
        _g = jnp.sign(_g) * jnp.maximum(jnp.abs(_g), 1.0) + (_g == 0) * 1.0
        g_xattn = _g[0]
        g_ffn = _g[1]
        return (x, ctx_4096, g_xattn, g_ffn)
    x, ctx_4096, g_xattn, g_ffn = _rec_inputs()

    def _L0_xattn_setup():
        import jax, jax.numpy as jnp
        import numpy as np
        import math
        D_MODEL = 256
        NHEAD = 16
        MAX_SUP = 4
        DK = D_MODEL // NHEAD
        DM = D_MODEL * MAX_SUP
        B, S = (2, 256)
        key = jax.random.key(seed)
        ks = jax.random.split(key, 12)
        std = 0.02
        inp = {'q': jax.random.normal(ks[0], (B, S, DM), jnp.float32), 'k': jax.random.normal(ks[1], (B, S, DM), jnp.float32), 'v': jax.random.normal(ks[2], (B, S, DM), jnp.float32), 'Wq': jax.random.normal(ks[3], (DM, DM), jnp.float32) * std, 'bq': jnp.zeros((DM,), jnp.float32), 'Wk': jax.random.normal(ks[4], (DM, DM), jnp.float32) * std, 'bk': jnp.zeros((DM,), jnp.float32), 'Wv': jax.random.normal(ks[5], (DM, DM), jnp.float32) * std, 'bv': jnp.zeros((DM,), jnp.float32), 'interference': jax.random.normal(ks[6], (NHEAD, MAX_SUP, MAX_SUP), jnp.float32), 'amp': jnp.ones((1,), jnp.float32), 'Wo': jax.random.normal(ks[7], (DM, DM), jnp.float32) * std, 'bo': jnp.zeros((DM,), jnp.float32)}
        return inp
    _L0_xattn_all = _L0_xattn_setup()
    _L0_xattn_in = {k: v for k, v in _L0_xattn_all.items() if k in ('Wq', 'bq', 'Wk', 'bk', 'Wv', 'bv', 'interference', 'amp', 'Wo', 'bo')}
    del _L0_xattn_all

    def _L0_ffn_setup():
        import jax, jax.numpy as jnp
        import numpy as np
        import math
        B, S, IN, OUT = (4, 512, 1024, 1024)
        E, R, K = (8, 64, 128)
        SCALE = 64.0 / 64.0
        MULTIPLIER = 1.0
        key = jax.random.key(seed)
        ks = jax.random.split(key, 6)
        return {'x': jax.random.normal(ks[0], (B, S, IN), jnp.float32), 'W_org': jax.random.normal(ks[1], (OUT, IN), jnp.float32) * 0.02, 'lora_down': jax.random.normal(ks[2], (E, IN, R), jnp.float32) * 0.02, 'lora_up': jax.random.normal(ks[3], (E, R, OUT), jnp.float32) * 0.02, 'lora_keys': jax.random.normal(ks[4], (E, K), jnp.float32), 'Wq': jax.random.normal(ks[5], (K, IN), jnp.float32) * 0.02}
    _L0_ffn_all = _L0_ffn_setup()
    _L0_ffn_in = {k: v for k, v in _L0_ffn_all.items() if k in ('W_org', 'lora_down', 'lora_up', 'lora_keys', 'Wq')}
    del _L0_ffn_all
    return {'x': x, 'ctx_4096': ctx_4096, 'g_xattn': g_xattn, 'g_ffn': g_ffn, 'L0_xattn_Wq': _L0_xattn_in['Wq'], 'L0_xattn_bq': _L0_xattn_in['bq'], 'L0_xattn_Wk': _L0_xattn_in['Wk'], 'L0_xattn_bk': _L0_xattn_in['bk'], 'L0_xattn_Wv': _L0_xattn_in['Wv'], 'L0_xattn_bv': _L0_xattn_in['bv'], 'L0_xattn_interference': _L0_xattn_in['interference'], 'L0_xattn_amp': _L0_xattn_in['amp'], 'L0_xattn_Wo': _L0_xattn_in['Wo'], 'L0_xattn_bo': _L0_xattn_in['bo'], 'L0_ffn_W_org': _L0_ffn_in['W_org'], 'L0_ffn_lora_down': _L0_ffn_in['lora_down'], 'L0_ffn_lora_up': _L0_ffn_in['lora_up'], 'L0_ffn_lora_keys': _L0_ffn_in['lora_keys'], 'L0_ffn_Wq': _L0_ffn_in['Wq']}

def reference(x, ctx_4096, g_xattn, g_ffn, L0_xattn_Wq, L0_xattn_bq, L0_xattn_Wk, L0_xattn_bk, L0_xattn_Wv, L0_xattn_bv, L0_xattn_interference, L0_xattn_amp, L0_xattn_Wo, L0_xattn_bo, L0_ffn_W_org, L0_ffn_lora_down, L0_ffn_lora_up, L0_ffn_lora_keys, L0_ffn_Wq):
    import jax
    import jax.numpy as jnp

    def _L0_xattn_ref(q, k, v, Wq, bq, Wk, bk, Wv, bv, interference, amp, Wo, bo):
        import jax, jax.numpy as jnp
        import numpy as np
        import math
        D_MODEL = 256
        NHEAD = 16
        MAX_SUP = 4
        DK = D_MODEL // NHEAD
        DM = D_MODEL * MAX_SUP
        B, S = (2, 256)
        b, s, dm = q.shape
        H, M = (interference.shape[0], interference.shape[1])
        dk = dm // (H * M)

        def proj(x, W, bias):
            y = x @ W.T + bias
            y = y.reshape(b, s, H, dk, M)
            return jnp.transpose(y, (0, 2, 1, 3, 4))
        qh = proj(q, Wq, bq)
        kh = proj(k, Wk, bk)
        vh = proj(v, Wv, bv)

        def interfere(x):
            return x + 0.1 * amp[0] * jnp.einsum('bhsdi,hij->bhsdj', x, interference)
        qh, kh, vh = (interfere(qh), interfere(kh), interfere(vh))
        scores = jnp.einsum('bhqdm,bhkdm->bhqkm', qh, kh) / math.sqrt(dk)
        weights = jax.nn.softmax(scores, axis=3)
        out = jnp.einsum('bhqkm,bhkdm->bhqdm', weights, vh)
        out = jnp.transpose(out, (0, 2, 1, 3, 4)).reshape(b, s, dm)
        return out @ Wo.T + bo

    def _L0_ffn_ref(x, W_org, lora_down, lora_up, lora_keys, Wq):
        import jax, jax.numpy as jnp
        import numpy as np
        import math
        B, S, IN, OUT = (4, 512, 1024, 1024)
        E, R, K = (8, 64, 128)
        SCALE = 64.0 / 64.0
        MULTIPLIER = 1.0
        base = jnp.einsum('bsi,oi->bso', x, W_org)
        q = jnp.einsum('bi,ki->bk', x.mean(axis=1), Wq)
        scores = jnp.einsum('bk,ek->be', q, lora_keys) / math.sqrt(K)
        coeffs = jax.nn.softmax(scores, axis=-1)
        h = jnp.einsum('bsi,eir->bser', x, lora_down)
        delta = jnp.einsum('be,bser,ero->bso', coeffs, h, lora_up)
        return base + delta * (SCALE * MULTIPLIER)
    x = x + jnp.tanh(g_xattn[0]) * _L0_xattn_ref(_layernorm(x, axis=-1), ctx_4096, ctx_4096, L0_xattn_Wq, L0_xattn_bq, L0_xattn_Wk, L0_xattn_bk, L0_xattn_Wv, L0_xattn_bv, L0_xattn_interference, L0_xattn_amp, L0_xattn_Wo, L0_xattn_bo)
    x = x + jnp.tanh(g_ffn[0]) * _L0_ffn_ref(_layernorm(x, axis=-1), L0_ffn_W_org, L0_ffn_lora_down, L0_ffn_lora_up, L0_ffn_lora_keys, L0_ffn_Wq)
    return x

_drawn_inputs = setup_inputs


def setup_inputs(seed=0):
    import zlib

    import numpy as np

    out = dict(_drawn_inputs(seed))
    spreads = {'L0_xattn_bq': (0.0, 0.8),
     'L0_xattn_bk': (0.0, 0.8),
     'L0_xattn_bv': (0.0, 0.1),
     'L0_xattn_bo': (0.0, 0.1)}
    factors = {'L0_ffn_lora_keys': 8.0, 'L0_ffn_Wq': 8.0}
    for name, (base, spread) in spreads.items():
        noise = np.random.default_rng([zlib.crc32(name.encode()), seed]).standard_normal(out[name].shape)
        drawn = base * np.exp(spread * noise) if base else spread * noise
        out[name] = jnp.asarray(drawn.astype(out[name].dtype))
    for name, factor in factors.items():
        out[name] = (out[name] * factor).astype(out[name].dtype)
    return out
```

```python
from contextlib import ExitStack

import concourse.bass as bass
from concourse import mybir

F32 = mybir.dt.float32
F32R = mybir.dt.float32r
ALU = mybir.AluOpType
ACT = mybir.ActivationFunctionType
AX = mybir.AxisListType

P = 128
EPS = 1e-5


class Job:

    def __init__(self, pe, dve, act=None, reads=0, pe_wait=None, act_wait=None, dve_wait=None,
                 act_pre=None, dve_pre=None):
        self.pe, self.dve, self.act, self.reads = pe, dve, act, reads
        self.pe_wait, self.act_wait, self.dve_wait = pe_wait, act_wait, dve_wait
        self.act_pre, self.dve_pre = act_pre, dve_pre


class Line:

    def __init__(self, banks, filled, scaled, emptied):
        self.banks, self.jobs = banks, []
        self.filled, self.scaled, self.emptied = filled, scaled, emptied

    def add(self, job):
        self.jobs.append(job)
        return len(self.jobs)

    def bank(self, n):
        return self.banks[n % len(self.banks)]

    def wait_filled(self, eng, end):
        eng.wait_ge(self.filled, sum(1 for job in self.jobs[:end] if job.pe))

    def run_tensor(self, pe):
        ring = len(self.banks)
        for n, job in enumerate(self.jobs):
            need = max(n + 1 - ring, job.reads, 0)
            if job.pe:
                if need:
                    pe.wait_ge(self.emptied, need)
                if job.pe_wait:
                    job.pe_wait(pe)
                job.pe(self.bank(n)).then_inc(self.filled, 1)

    def run_scalar(self, act):
        for n, job in enumerate(self.jobs):
            if job.act_pre:
                job.act_pre(act)
            if job.act:
                if job.pe:
                    self.wait_filled(act, n + 1)
                if job.act_wait:
                    job.act_wait(act)
                job.act(self.bank(n)).then_inc(self.scaled, 1)

    def run_vector(self, dve):
        scaled = 0
        for n, job in enumerate(self.jobs):
            if job.dve_pre:
                job.dve_pre(dve)
            if job.act:
                scaled += 1
                dve.wait_ge(self.scaled, scaled)
            else:
                self.wait_filled(dve, n + 1)
            if job.dve_wait:
                job.dve_wait(dve)
            job.dve(self.bank(n)).then_inc(self.emptied, 1)


def build(nc, x, ctx_in, g_xattn, g_ffn, wq, bq, wk, bk, wv, bv, interference, amp, wo, bo,
          w_org, lora_down, lora_up, lora_keys, w_key, out):
    NB, S, D = x.shape
    NH, NM, _ = interference.shape
    DK = D // (NH * NM)
    HM = NH * NM
    NE, _, R = lora_down.shape
    NK = w_key.shape[0]
    T = NB * S
    KC = D // P
    GB = 4
    NG = NB // GB
    GT = GB * S
    HALF = 512
    LC = NE * R // P
    STACK = 3 * DK
    OCT = P // DK
    NOCT = HM // OCT
    PAIRS = HM // 2
    assert S == P and OCT == 8 and T % GT == 0

    x_t = x.rearrange("b s d -> (b s) d")
    ctx_t = ctx_in.rearrange("b s d -> (b s) d")
    out_t = out.rearrange("b s d -> (b s) d")

    k_stack = nc.dram_tensor("k_stack", (HM, 3, DK, T), F32, kind="Internal").ap()
    q_stack = nc.dram_tensor("q_stack", (HM, 3, DK, T), F32, kind="Internal").ap()
    v_pad = nc.dram_tensor("v_pad", (T, PAIRS * 2 * 32), F32, kind="Internal").ap()
    x_bias = nc.dram_tensor("x_bias", (T, D), F32, kind="Internal").ap()
    x_mid = nc.dram_tensor("x_mid", (T, D), F32, kind="Internal").ap()

    top = ExitStack()
    with top:
        def sem(name):
            return top.enter_context(nc.semaphore(name))

        def sb(name, shape, dt=F32, stack=top):
            return stack.enter_context(nc.sbuf_tensor(name, shape, dt))

        banks = [top.enter_context(nc.psum_tensor(f"bank{i}", [P, HALF], F32)) for i in range(8)]

        ident = sb("ident", [P, P])
        ln2_stats = sb("ln2_stats", [P, NB, 2, 6])
        gates = sb("gates", [P, 2])
        s_const = sem("s_const")
        s_chain = sem("s_chain")
        chain = [0]

        def link(ins):
            chain[0] += 1
            ins.then_inc(s_chain, 1)
            nc.vector.wait_ge(s_chain, chain[0])

        def split_hi(hi, bank_ap, **kw):
            return nc.scalar.activation(hi, bank_ap, ACT.Copy, **kw)

        def split_lo(lo, bank_ap, hi):
            return nc.vector.tensor_tensor(lo, bank_ap, hi.bitcast(F32), ALU.subtract)

        def three_products(bank_ap, station, moving, chunks):
            last = None
            for i, k in enumerate(chunks):
                (sh, sl), (mh, ml) = station(k), moving(k)
                nc.tensor.matmul(bank_ap, sh, mh, start=(i == 0), stop=False)
                nc.tensor.matmul(bank_ap, sh, ml, start=False, stop=False)
                last = nc.tensor.matmul(bank_ap, sl, mh, start=False, stop=(i == len(chunks) - 1))
            return last

        proj = ExitStack()
        mix = sb("mix", [P, KC, P], stack=proj)
        bias_mixed = sb("bias_mixed", [P, 2, KC], stack=proj)
        ctx_a = ExitStack()
        bv_row = sb("bv_row", [P, D], stack=ctx_a)

        with ExitStack() as st, nc.Block() as block:
            jm = sb("jm", [NM, NH, NM], stack=st)
            amp4 = sb("amp4", [NM, 1], stack=st)
            braw = sb("braw", [3 * KC, P], stack=st)
            graw = sb("graw", [P, 2], stack=st)
            rowsel = sb("rowsel", [NM, P // NM, NM], stack=st)
            jrow = sb("jrow", [P, NH, NM], stack=st)
            group = sb("group", [P, P // NM], stack=st)
            bcol = sb("bcol", [P, 3 * KC], stack=st)
            bvb = sb("bvb", [P, KC, P], stack=st)
            s_in, s_id, s_ready, s_mm, s_g = (sem(n) for n in ("s_in", "s_id", "s_ready", "s_mm", "s_g"))

            @block.sync
            def _(sp):
                with nc.allow_non_contiguous_dma(reason="a few hundred small elements"):
                    sp.dma_start(jm[:], interference.rearrange("h i j -> i h j")).then_inc(s_in, 16)
                    sp.dma_start(amp4[:], amp.partition_broadcast(NM)).then_inc(s_in, 16)
                    sp.dma_start(graw[:, 0:1], g_xattn.partition_broadcast(P)).then_inc(s_in, 16)
                    sp.dma_start(graw[:, 1:2], g_ffn.partition_broadcast(P)).then_inc(s_in, 16)
                    for i, b in enumerate((bk, bq, bv)):
                        sp.dma_start(braw[i * KC:(i + 1) * KC, :],
                                     b.rearrange("(c i) -> c i", i=P)).then_inc(s_in, 16)

            @block.gpsimd
            def _(pool):
                pool.memset(ident[:], 0.0).then_inc(s_id, 1)
                pool.wait_ge(s_id, 1)
                pool.affine_select(out=ident[:], in_=ident[:], compare_op=ALU.not_equal, fill=1.0, base=0,
                                   pattern=[[-1, P]], channel_multiplier=1).then_inc(s_id, 1)

            @block.scalar
            def _(act):
                act.wait_ge(s_in, 7 * 16)
                act.activation(gates[:], graw[:], ACT.Tanh).then_inc(s_g, 1)

            @block.vector
            def _(dve):
                dve.wait_ge(s_in, 7 * 16)
                dve.wait_ge(s_id, 2)
                dve.tensor_copy(rowsel[:], ident[0:NM, 0:NM].unsqueeze(1).to_broadcast([NM, P // NM, NM]))
                dve.tensor_reduce(group[:], ident[:].rearrange("p (g f) -> p g f", f=NM), AX.X, ALU.add)
                link(dve.tensor_scalar(jm[:], jm[:], amp4[:, 0:1], 0.1, ALU.mult, ALU.mult))
                link(dve.tensor_tensor(jm[:], jm[:],
                                       ident[0:NM, 0:NM].unsqueeze(1).to_broadcast([NM, NH, NM]), ALU.add))
                dve.sem_inc(s_ready, 1)
                dve.wait_ge(s_mm, 2)
                dve.tensor_copy(jrow[:].rearrange("p h m -> p (h m)"), banks[0][:, 0:HM])
                link(dve.tensor_copy(bcol[:], banks[1][:, 0:3 * KC]))
                for c in range(KC):
                    for h2 in range(2):
                        width = P // 2
                        dst = mix[:, c, h2 * width:(h2 + 1) * width].rearrange("p (m d) -> p m d", m=NM)
                        dve.tensor_tensor(
                            dst, jrow[:, 2 * c + h2, :].unsqueeze(2).to_broadcast([P, NM, DK]),
                            group[:, h2 * DK:(h2 + 1) * DK].unsqueeze(1).to_broadcast([P, NM, DK]), ALU.mult)
                link(dve.tensor_copy(bvb[:], bcol[:, 2 * KC:3 * KC].unsqueeze(2).to_broadcast([P, KC, P])))
                dve.sem_inc(s_ready, 1)
                dve.wait_ge(s_mm, 3)
                dve.tensor_copy(bias_mixed[:].rearrange("p a c -> p (a c)"), banks[2][:, 0:2 * KC])
                dve.tensor_copy(bv_row[:, 0:HALF], banks[3][:])
                link(dve.tensor_copy(bv_row[:, HALF:D], banks[4][:]))

            @block.tensor
            def _(pe):
                pe.wait_ge(s_ready, 1)
                pe.wait_ge(s_in, 7 * 16)
                pe.matmul(banks[0][:, 0:HM], rowsel[:].rearrange("m g f -> m (g f)"),
                          jm[:].rearrange("i h j -> i (h j)"), start=True, stop=True).then_inc(s_mm, 1)
                pe.transpose(banks[1][:, 0:3 * KC], braw[:], ident[0:3 * KC, 0:3 * KC]).then_inc(s_mm, 1)
                pe.wait_ge(s_ready, 2)
                for a in range(2):
                    for c in range(KC):
                        pe.matmul(banks[2][:, a * KC + c:a * KC + c + 1], mix[:, c, :],
                                  bcol[:, a * KC + c:a * KC + c + 1], start=True, stop=True)
                for c in range(KC):
                    last = pe.matmul(banks[3 + c // 4][:, (c % 4) * P:(c % 4 + 1) * P], bvb[:, c, :],
                                     mix[:, c, :], start=True, stop=True)
                last.then_inc(s_mm, 1)

        def weight_jobs(line, w, w_hi, w_lo, raw, s_raw, plan, mixed=None, permuted=None):
            ring = len(raw)
            done_with = []
            for c in range(w.shape[0] // P):
                slot, use = c % ring, raw_uses[0]
                raw_uses[0] += 1
                slot = use % ring
                free = last_raw_user.get(slot, 0)

                def load(sp, c=c, slot=slot, free=free):
                    if free:
                        line.wait_filled(sp, free)
                    sp.dma_start(raw[slot][:], w[c * P:(c + 1) * P, :]).then_inc(s_raw[slot], 16)

                plan.append((free - 0.5, load))
                for half in range(2):
                    def pe_fn(bank, c=c, half=half, slot=slot):
                        last = None
                        for q in range(4):
                            k = 4 * half + q
                            rows = (permuted[0][c] if permuted else raw[slot])[:, k * P:(k + 1) * P]
                            dst = bank[:, q * P:(q + 1) * P]
                            if mixed is not None:
                                last = nc.tensor.matmul(dst, rows, mixed[:, c, :], start=True, stop=True)
                            else:
                                last = nc.tensor.transpose(dst, rows, ident[:])
                        return last

                    hi = w_hi[:, 4 * half:4 * half + 4, c * P:(c + 1) * P]
                    lo = w_lo[:, 4 * half:4 * half + 4, c * P:(c + 1) * P]

                    def wait_raw(pe, c=c, slot=slot, n=use // ring + 1):
                        if permuted:
                            pe.wait_ge(permuted[1], c + 1)
                        else:
                            pe.wait_ge(s_raw[slot], 16 * n)

                    end = line.add(Job(
                        pe_fn, lambda bank, hi=hi, lo=lo: split_lo(lo, bank[:].rearrange("p (q r) -> p q r", q=4), hi),
                        act=lambda bank, hi=hi: split_hi(hi, bank[:].rearrange("p (q r) -> p q r", q=4)),
                        pe_wait=wait_raw))
                last_raw_user[slot] = end
            return end

        def run_phase(block, line, plan, stores_end=None):
            @block.sync
            def _(sp):
                for _, step in sorted(plan, key=lambda e: e[0]):
                    step(sp)
                if stores_end:
                    stores_end(sp)

            @block.tensor
            def _(pe):
                line.run_tensor(pe)

            @block.scalar
            def _(act):
                line.run_scalar(act)

            @block.vector
            def _(dve):
                line.run_vector(dve)

        def new_line(tag):
            return Line(banks, sem(f"s_filled_{tag}"), sem(f"s_scaled_{tag}"), sem(f"s_emptied_{tag}"))

        def stacked(scratch, c, section, g):
            return scratch[c * OCT:(c + 1) * OCT, section, :, g * GT:(g + 1) * GT]

        def projection_store(line, plan, scratch, hi, lo, s_free, c, g, end, hi_sections, lo_section):
            def store(sp):
                sp.wait_ge(line.emptied, end)
                for section in range(3):
                    src = lo if section == lo_section else hi
                    sp.dma_start(stacked(scratch, c, section, g), src[:].bitcast(F32)).then_inc(s_free, 16)
            plan.append((end + 0.6, store))

        with ExitStack() as st, nc.Block() as block:
            wk_hi, wk_lo, wv_hi, wv_lo = (sb(n, [P, KC, D], F32R, st) for n in ("wk_hi", "wk_lo", "wv_hi", "wv_lo"))
            cT_hi = sb("cT_hi", [P, GB, KC, P], F32R, st)
            cT_lo = sb("cT_lo", [P, GB, KC, P], F32R, st)
            raw = [sb(f"raw_a{i}", [P, D], F32, st) for i in range(2)]
            cin = [sb(f"cin{i}", [P, D], F32, st) for i in range(2)]
            k_hi = [sb(f"k_hi{i}", [P, GT], F32R, st) for i in range(2)]
            k_lo = [sb(f"k_lo{i}", [P, GT], F32R, st) for i in range(2)]
            v_out = [sb(f"v_out{i}", [P, PAIRS // 2, 2, 32], F32, st) for i in range(2)]
            s_raw = [sem(f"s_raw_a{i}") for i in range(2)]
            s_cin = [sem(f"s_cin{i}") for i in range(2)]
            s_kst = [sem(f"s_kst{i}") for i in range(2)]
            s_vst = [sem(f"s_vst{i}") for i in range(2)]
            line, plan = new_line("a"), []
            raw_uses, last_raw_user = [0], {}
            t_end = {}

            def ctx_jobs(b):
                slot, gslot = b % 2, b % GB
                free = t_end.get(b - 2, 0)

                def load(sp, b=b):
                    if free:
                        line.wait_filled(sp, free)
                    sp.dma_start(cin[slot][:], ctx_t[b * P:(b + 1) * P, :]).then_inc(s_cin[slot], 16)
                plan.append((free - 0.5, load))
                for half in range(2):
                    def pe_fn(bank, half=half):
                        for q in range(4):
                            k = 4 * half + q
                            last = nc.tensor.transpose(bank[:, q * P:(q + 1) * P], cin[slot][:, k * P:(k + 1) * P], ident[:])
                        return last
                    hi = cT_hi[:, gslot, 4 * half:4 * half + 4, :].rearrange("p a b -> p (a b)")
                    lo = cT_lo[:, gslot, 4 * half:4 * half + 4, :].rearrange("p a b -> p (a b)")
                    t_end[b] = line.add(Job(
                        pe_fn, lambda bank, hi=hi, lo=lo: split_lo(lo, bank[:], hi),
                        act=lambda bank, hi=hi: split_hi(hi, bank[:]),
                        pe_wait=lambda pe: pe.wait_ge(s_cin[slot], 16 * (b // 2 + 1))))

            def k_job(g, c):
                n = g * KC + c
                slot, use = n % 2, n // 2
                bias = bias_mixed[:, 0, c:c + 1]
                hi, lo = k_hi[slot], k_lo[slot]

                def pe_fn(bank):
                    return three_products(
                        bank[:], lambda k: (wk_hi[:, k, c * P:(c + 1) * P], wk_lo[:, k, c * P:(c + 1) * P]),
                        lambda k: (cT_hi[:, :, k, :], cT_lo[:, :, k, :]), range(KC))

                def stage_free(act):
                    if use:
                        act.wait_ge(s_kst[slot], 48 * use)
                end = line.add(Job(
                    pe_fn,
                    lambda bank: nc.vector.scalar_tensor_tensor(
                        out=lo[:], in0=bank[:], scalar=bias, in1=hi[:].bitcast(F32), op0=ALU.add, op1=ALU.subtract),
                    act=lambda bank: nc.scalar.activation(hi[:], bank[:], ACT.Identity, bias=bias),
                    reads=max(t_end[g * GB + GB - 1], wk_end), act_wait=stage_free))
                projection_store(line, plan, k_stack, hi, lo, s_kst[slot], c, g, end, (0, 1), 2)

            def v_job(b, half):
                n = 2 * b + half
                slot, use = n % 2, n // 2
                gslot = b % GB

                def pe_fn(bank):
                    return three_products(
                        bank[:], lambda k: (cT_hi[:, gslot, k, :], cT_lo[:, gslot, k, :]),
                        lambda k: (wv_hi[:, k, half * HALF:(half + 1) * HALF], wv_lo[:, k, half * HALF:(half + 1) * HALF]),
                        range(KC))

                def empty(bank):
                    last = None
                    for ab in range(2):
                        last = nc.vector.tensor_tensor(
                            v_out[slot][:, :, ab, ab * DK:(ab + 1) * DK],
                            bank[:].rearrange("p (q a d) -> p q a d", a=2, d=DK)[:, :, ab, :],
                            bv_row[:, half * HALF:(half + 1) * HALF].rearrange("p (q a d) -> p q a d", a=2, d=DK)[:, :, ab, :],
                            ALU.add)
                    return last

                def stage_free(dve):
                    if use:
                        dve.wait_ge(s_vst[slot], 16 * use)
                end = line.add(Job(pe_fn, empty, reads=max(t_end[b], wv_end), dve_wait=stage_free))

                def store(sp):
                    sp.wait_ge(line.emptied, end)
                    width = PAIRS * 32
                    sp.dma_start(v_pad[b * P:(b + 1) * P, half * width:(half + 1) * width],
                                 v_out[slot][:].rearrange("p q a d -> p (q a d)")).then_inc(s_vst[slot], 16)
                plan.append((end + 0.6, store))

            wk_end = weight_jobs(line, wk, wk_hi, wk_lo, raw, s_raw, plan, mixed=mix)
            for b in range(GB):
                ctx_jobs(b)
            for c in range(KC):
                k_job(0, c)
            wv_end = weight_jobs(line, wv, wv_hi, wv_lo, raw, s_raw, plan, mixed=mix)
            for g in range(NG):
                for b in range(g * GB, (g + 1) * GB):
                    v_job(b, 0)
                    v_job(b, 1)
                    if g + 1 < NG:
                        ctx_jobs(b + GB)
                if g + 1 < NG:
                    for c in range(KC):
                        k_job(g + 1, c)

            for i in range(2):
                line.jobs[i].dve_pre = lambda dve, i=i: link(dve.memset(v_out[i][:], 0.0))

            def stores_end(sp):
                for i in range(2):
                    sp.wait_ge(s_kst[i], 48 * (NG * KC // 2))
                    sp.wait_ge(s_vst[i], 16 * NB)
            run_phase(block, line, plan, stores_end)
        ctx_a.close()

        with ExitStack() as st, nc.Block() as block:
            wq_hi, wq_lo = (sb(n, [P, KC, D], F32R, st) for n in ("wq_hi", "wq_lo"))
            xT_hi = [sb(f"xT_hi{i}", [P, GB, KC, P], F32R, st) for i in range(2)]
            xT_lo = [sb(f"xT_lo{i}", [P, GB, KC, P], F32R, st) for i in range(2)]
            raw = [sb(f"raw_b{i}", [P, D], F32, st) for i in range(2)]
            xin = [sb(f"xin{i}", [P, D], F32, st) for i in range(GB)]
            xn = [sb(f"xn{i}", [P, D], F32, st) for i in range(GB)]
            q_hi = [sb(f"q_hi{i}", [P, GT], F32R, st) for i in range(2)]
            q_lo = [sb(f"q_lo{i}", [P, GT], F32R, st) for i in range(2)]
            bo_row = sb("bo_row", [P, D], F32, st)
            stats = sb("stats", [P, GB, 2, 6], F32, st)
            mv = sb("mv", [P, GB, 2], F32, st)
            root = sb("root", [P, GB], F32, st)
            rstd = sb("rstd", [P, GB], F32, st)
            tmp = sb("tmp", [P, GB], F32, st)
            s_raw = [sem(f"s_raw_b{i}") for i in range(2)]
            s_xin = [sem(f"s_xin{i}") for i in range(GB)]
            s_qst = [sem(f"s_qst{i}") for i in range(2)]
            s_xb = [sem(f"s_xb{i}") for i in range(GB)]
            s_bo, s_stat, s_root, s_xn = (sem(n) for n in ("s_bo", "s_stat", "s_root", "s_xn"))
            line, plan = new_line("b"), []
            raw_uses, last_raw_user = [0], {}
            t_end = {}

            def inverse_root(dve, var, root, rstd, tmp):
                link(dve.reciprocal(rstd, root))
                link(dve.tensor_tensor(tmp, rstd, rstd, ALU.mult))
                link(dve.tensor_tensor(tmp, tmp, var, ALU.mult))
                link(dve.tensor_scalar(tmp, tmp, -0.5, 1.5, ALU.mult, ALU.add))
                link(dve.tensor_tensor(rstd, rstd, tmp, ALU.mult))

            def load_bo(sp):
                sp.dma_start(bo_row[:], bo.partition_broadcast(P)).then_inc(s_bo, 16)
            plan.append((-0.7, load_bo))

            def load_x(b):
                slot = b % GB

                def load(sp):
                    if b >= GB:
                        sp.wait_ge(s_xn, b - GB + 1)
                        sp.wait_ge(s_xb[slot], 16 * (b // GB))
                    sp.dma_start(xin[slot][:], x_t[b * P:(b + 1) * P, :]).then_inc(s_xin[slot], 16)
                return load

            def stats_of(g):
                def pre(dve):
                    if g == 0:
                        dve.wait_ge(s_bo, 16)
                        link(dve.tensor_scalar(bo_row[:], bo_row[:], gates[:, 0:1], None, ALU.mult))
                    for i in range(GB):
                        dve.wait_ge(s_xin[i], 16 * (g + 1))
                        for h in range(2):
                            last = dve.bn_stats(stats[:, i, h, :], xin[i][:, h * HALF:(h + 1) * HALF])
                    link(last)
                    for i in range(GB):
                        last = dve.bn_aggr(mv[:, i, :], stats[:, i, :, :])
                    link(last)
                    link(dve.tensor_scalar(mv[:, :, 1:2], mv[:, :, 1:2], EPS, None, ALU.add))
                    dve.sem_inc(s_stat, 1)
                return pre

            def root_of(g):
                def pre(act):
                    act.wait_ge(s_stat, g + 1)
                    act.activation(root[:], mv[:, :, 1:2].rearrange("p a b -> p (a b)"), ACT.Sqrt).then_inc(s_root, 1)
                return pre

            def normalise(g):
                def pre(dve):
                    dve.wait_ge(s_root, g + 1)
                    inverse_root(dve, mv[:, :, 1:2].rearrange("p a b -> p (a b)"), root[:], rstd[:], tmp[:])
                    for i in range(GB):
                        b = g * GB + i
                        if g:
                            line.wait_filled(dve, t_end[b - GB])
                        dve.tensor_scalar(xn[i][:], xin[i][:], mv[:, i, 0:1], rstd[:, i:i + 1],
                                          ALU.subtract, ALU.mult)
                        link(dve.tensor_tensor(xin[i][:], xin[i][:], bo_row[:], ALU.add))
                        dve.sem_inc(s_xn, 1)
                return pre

            def store_xb(b):
                def store(sp):
                    sp.wait_ge(s_xn, b + 1)
                    sp.dma_start(x_bias[b * P:(b + 1) * P, :], xin[b % GB][:]).then_inc(s_xb[b % GB], 16)
                return store

            def t_jobs(b):
                g, i = b // GB, b % GB
                for half in range(2):
                    def pe_fn(bank, half=half):
                        for q in range(4):
                            k = 4 * half + q
                            last = nc.tensor.transpose(bank[:, q * P:(q + 1) * P], xn[i][:, k * P:(k + 1) * P], ident[:])
                        return last
                    hi = xT_hi[g % 2][:, i, 4 * half:4 * half + 4, :].rearrange("p a b -> p (a b)")
                    lo = xT_lo[g % 2][:, i, 4 * half:4 * half + 4, :].rearrange("p a b -> p (a b)")
                    t_end[b] = line.add(Job(
                        pe_fn, lambda bank, hi=hi, lo=lo: split_lo(lo, bank[:], hi),
                        act=lambda bank, hi=hi: split_hi(hi, bank[:]),
                        pe_wait=lambda pe: pe.wait_ge(s_xn, b + 1)))

            def q_job(g, c):
                n = g * KC + c
                slot, use = n % 2, n // 2
                bias = q_bias[:, c:c + 1]
                hi, lo = q_hi[slot], q_lo[slot]

                def pe_fn(bank):
                    return three_products(
                        bank[:], lambda k: (wq_hi[:, k, c * P:(c + 1) * P], wq_lo[:, k, c * P:(c + 1) * P]),
                        lambda k: (xT_hi[g % 2][:, :, k, :], xT_lo[g % 2][:, :, k, :]), range(KC))

                def stage_free(act):
                    if use:
                        act.wait_ge(s_qst[slot], 48 * use)
                job = Job(
                    pe_fn,
                    lambda bank: nc.vector.scalar_tensor_tensor(
                        out=lo[:], in0=bank[:], scalar=bias, in1=hi[:].bitcast(F32), op0=ALU.add, op1=ALU.subtract),
                    act=lambda bank: nc.scalar.activation(hi[:], bank[:], ACT.Identity, bias=bias),
                    reads=max(t_end[g * GB + GB - 1], wq_end), act_wait=stage_free)
                end = line.add(job)
                projection_store(line, plan, q_stack, hi, lo, s_qst[slot], c, g, end, (0, 2), 1)
                return job

            q_bias = bias_mixed[:, 1, :]
            wq_end = weight_jobs(line, wq, wq_hi, wq_lo, raw, s_raw, plan, mixed=mix)
            for b in range(GB):
                plan.append((-0.6, load_x(b)))
                plan.append((15.5, store_xb(b)))
            line.jobs[4].dve_pre, line.jobs[5].act_pre, line.jobs[9].dve_pre = stats_of(0), root_of(0), normalise(0)
            for b in range(GB):
                plan.append((15.6, load_x(b + GB)))
            for b in range(GB):
                t_jobs(b)
            for g in range(NG):
                for c in range(KC):
                    job = q_job(g, c)
                    if g + 1 < NG:
                        if c == 0:
                            job.dve_pre = stats_of(g + 1)
                        if c == 1:
                            job.act_pre, job.dve_pre = root_of(g + 1), normalise(g + 1)
                            at = len(line.jobs)
                            for b in range((g + 1) * GB, (g + 2) * GB):
                                plan.append((at + 0.7, store_xb(b)))
                                if b + GB < NB:
                                    plan.append((at + 0.8, load_x(b + GB)))
                        if 3 <= c < 3 + GB:
                            t_jobs((g + 1) * GB + c - 3)

            def stores_end(sp):
                for i in range(2):
                    sp.wait_ge(s_qst[i], 48 * (NG * KC // 2))
                for i in range(GB):
                    sp.wait_ge(s_xb[i], 16 * NG)
            run_phase(block, line, plan, stores_end)
        proj.close()

        phase_c = ExitStack()
        wo_hi, wo_lo = (sb(n, [P, KC, D], F32R, phase_c) for n in ("wo_hi", "wo_lo"))
        with ExitStack() as st, nc.Block() as block:
            raw = [sb(f"raw_c{i}", [P, D], F32, st) for i in range(KC)]
            perm = [sb(f"perm{i}", [P, D], F32, st) for i in range(KC)]
            s_raw = [sem(f"s_raw_c{i}") for i in range(KC)]
            s_perm = sem("s_perm")
            line, plan = new_line("w"), []
            raw_uses, last_raw_user = [0], {}
            weight_jobs(line, wo, wo_hi, wo_lo, raw, s_raw, plan, permuted=(perm, s_perm))

            def reorder(dve, c):
                dve.wait_ge(s_raw[c], 16)
                for m in range(NM):
                    last = dve.tensor_copy(perm[c][:].rearrange("p (h m d) -> p h m d", h=NH, m=NM)[:, :, m, :],
                                           raw[c][:].rearrange("p (h d m) -> p h m d", h=NH, m=NM)[:, :, m, :])
                last.then_inc(s_perm, 1)
            for c in range(KC):
                at = line.jobs[max(2 * c - 2, 0)]
                at.dve_pre = (lambda dve: (reorder(dve, 0), reorder(dve, 1))) if c < 2 else (
                    lambda dve, c=c: reorder(dve, c))
            run_phase(block, line, plan)

        with phase_c, ExitStack() as st, nc.Block() as block:
            KQ = 4
            q_in = [sb(f"q_in{i}", [2 * STACK, 4, P], F32R, st) for i in range(KQ)]
            k_in = [sb(f"k_in{i}", [2 * STACK, 4, 2, P], F32R, st) for i in range(KQ)]
            v_in = [sb(f"v_in{i}", [P, PAIRS, 2, 32], F32, st) for i in range(2)]
            NP = 3
            prob = [sb(f"prob{i}", [P, 4, P], F32, st) for i in range(NP)]
            probT = [sb(f"probT{i}", [P, OCT, P], F32, st) for i in range(2)]
            NS = 4
            negmax = sb("negmax", [P, NS, 4], F32, st)
            total = sb("total", [P, NS, 4], F32, st)
            rec = sb("rec", [P, NS, 4], F32, st)
            oT_hi = [sb(f"oT_hi{i}", [P, NOCT, P], F32R, st) for i in range(2)]
            oT_lo = [sb(f"oT_lo{i}", [P, NOCT, P], F32R, st) for i in range(2)]
            xb = [sb(f"xb{i}", [P, D], F32, st) for i in range(2)]
            x2 = [sb(f"x2_{i}", [P, D], F32, st) for i in range(2)]
            sc_bank, pt_bank, pv_bank, o_bank = banks[0:2], banks[2:4], banks[4:6], banks[6:8]

            s_kq = [sem(f"s_kq{i}") for i in range(KQ)]
            s_v = [sem(f"s_v{i}") for i in range(2)]
            s_xb = [sem(f"s_xb2_{i}") for i in range(2)]
            s_x2st = [sem(f"s_x2st{i}") for i in range(2)]
            (s_zero, s_score, s_max, s_exp, s_rec, s_norm, s_pt, s_ptc, s_pv, s_ohi, s_olo, s_o, s_x2) = (
                sem(n) for n in ("s_zero", "s_score", "s_max", "s_exp", "s_rec", "s_norm", "s_pt", "s_ptc",
                                 "s_pv", "s_ohi", "s_olo", "s_o", "s_x2"))

            QUADS = NB * HM // 4
            QB = HM // 4
            OCTS = NB * NOCT
            EV_AT = 12
            O_AT = 22
            STEPS = QB * (NB - 1) + O_AT + 2 * KC + 1

            def oct_in_pv(t):
                return (t - 5) // 2 if t >= 5 and t % 2 and (t - 5) // 2 < OCTS else None

            def half_in_ev(t):
                h = (t - EV_AT) // 8
                return h if t >= EV_AT and (t - EV_AT) % 8 == 0 and h < 2 * NB else None

            def chunk_in_o(t):
                j = t - O_AT
                return (j // QB, j % QB // KC, j % KC) if 0 <= j < QB * NB else None

            @block.sync
            def _(sp):
                sp.wait_ge(s_zero, 1)

                def load_oct(o):
                    slot, b, first = o % KQ, o // NOCT, (o % NOCT) * OCT
                    if o >= KQ:
                        sp.wait_ge(s_score, 2 * (o - KQ) + 2)
                    tok = slice(b * P, (b + 1) * P)
                    sp.dma_start(
                        q_in[slot][:].bitcast(F32),
                        q_stack[first:first + OCT, :, :, tok].rearrange("(p a) s d t -> (a s d) p t", a=2)
                    ).then_inc(s_kq[slot], 16)
                    for a in range(2):
                        sp.dma_start(
                            k_in[slot][a * STACK:(a + 1) * STACK, :, a, :].bitcast(F32),
                            k_stack[first + a:first + OCT:2, :, :, tok].rearrange("p s d t -> (s d) p t")
                        ).then_inc(s_kq[slot], 16)

                def load_v(b):
                    if b >= 2:
                        sp.wait_ge(s_pv, NOCT * (b - 1))
                    sp.dma_start(v_in[b % 2][:].rearrange("p q a d -> p (q a d)"),
                                 v_pad[b * P:(b + 1) * P, :]).then_inc(s_v[b % 2], 16)

                def store_x2(b):
                    sp.wait_ge(s_x2, 2 * b + 2)
                    sp.dma_start(x_mid[b * P:(b + 1) * P, :], x2[b % 2][:]).then_inc(s_x2st[b % 2], 16)

                def load_xb(b):
                    sp.dma_start(xb[b % 2][:], x_bias[b * P:(b + 1) * P, :]).then_inc(s_xb[b % 2], 16)

                for o in range(OCTS):
                    b = o // NOCT
                    load_oct(o)
                    if o % NOCT == 1:
                        load_v(b)
                    if o % NOCT == NOCT - 1:
                        if b >= 2:
                            store_x2(b - 2)
                        load_xb(b)
                store_x2(NB - 2)
                store_x2(NB - 1)
                for i in range(2):
                    sp.wait_ge(s_x2st[i], 16 * (NB // 2))

            @block.tensor
            def _(pe):
                for t in range(STEPS):
                    if t < QUADS:
                        o, slot = t // 2, t // 2 % KQ
                        if t % 2 == 0:
                            pe.wait_ge(s_kq[slot], 48 * (o // KQ + 1))
                        if t >= 2:
                            pe.wait_ge(s_exp, t - 1)
                        for i in range(2):
                            p = 2 * (t % 2) + i
                            last = pe.matmul(sc_bank[t % 2][:, i * 2 * P:(i + 1) * 2 * P], q_in[slot][:, p, :],
                                             k_in[slot][:, p, :, :].rearrange("r a k -> r (a k)"), start=True, stop=True)
                        last.then_inc(s_score, 1)
                    if chunk_in_o(t):
                        b, half, k = chunk_in_o(t)
                        if k == 0:
                            pe.wait_ge(s_olo, 2 * b + 2)
                            if b:
                                pe.wait_ge(s_x2, 2 * (b - 1) + half + 1)
                        bank, cols = o_bank[half], slice(half * HALF, (half + 1) * HALF)
                        hi, lo = oT_hi[b % 2], oT_lo[b % 2]
                        pe.matmul(bank[:], hi[:, k, :], wo_hi[:, k, cols], start=(k == 0), stop=False)
                        pe.matmul(bank[:], hi[:, k, :], wo_lo[:, k, cols], start=False, stop=False)
                        last = pe.matmul(bank[:], lo[:, k, :], wo_hi[:, k, cols], start=False, stop=(k == KC - 1))
                        if k == KC - 1:
                            last.then_inc(s_o, 1)
                    if 2 <= t < QUADS + 2:
                        u = t - 2
                        pe.wait_ge(s_norm, u + 1)
                        if u >= 2:
                            pe.wait_ge(s_ptc, u - 1)
                        for j in range(4):
                            last = pe.transpose(pt_bank[u % 2][:, j * P:(j + 1) * P], prob[u % NP][:, j, :], ident[:])
                        last.then_inc(s_pt, 1)
                    if oct_in_pv(t) is not None:
                        o = oct_in_pv(t)
                        b, h = o // NOCT, o // 4
                        pe.wait_ge(s_ptc, 2 * o + 2)
                        if o % NOCT == 0:
                            pe.wait_ge(s_v[b % 2], 16 * (b // 2 + 1))
                        if o % 4 == 0 and h >= 2:
                            pe.wait_ge(s_olo, h - 1)
                        for a in range(2):
                            for p in range(4):
                                last = pe.matmul(
                                    pv_bank[h % 2][32 * p:32 * p + 32, (o % 4) * P:(o % 4 + 1) * P],
                                    v_in[b % 2][:, 4 * (o % NOCT) + p, a, :], probT[o % 2][:, 2 * p + a, :],
                                    start=(a == 0), stop=(a == 1), skip_group_check=True)
                        last.then_inc(s_pv, 1)

            @block.scalar
            def _(act):
                for t in range(STEPS):
                    if t < QUADS:
                        act.wait_ge(s_max, t + 1)
                        if t >= NP:
                            act.wait_ge(s_pt, t - NP + 1)
                        for j in range(4):
                            last = act.activation(prob[t % NP][:, j, :], sc_bank[t % 2][:, j * P:(j + 1) * P], ACT.Exp,
                                                  bias=negmax[:, t % NS, j:j + 1], scale=DK ** -0.5,
                                                  accum_out=total[:, t % NS, j:j + 1])
                        last.then_inc(s_exp, 1)
                    if half_in_ev(t) is not None:
                        h = half_in_ev(t)
                        b = h // 2
                        act.wait_ge(s_pv, 4 * h + 4)
                        if b >= 2:
                            act.wait_ge(s_o, 2 * (b - 1))
                        act.activation(oT_hi[b % 2][:, 4 * (h % 2):4 * (h % 2) + 4, :].rearrange("p a b -> p (a b)"),
                                       pv_bank[h % 2][:], ACT.Copy).then_inc(s_ohi, 1)

            @block.vector
            def _(dve):
                for i in range(KQ):
                    last = dve.memset(k_in[i][:].bitcast(F32), 0.0)
                last.then_inc(s_zero, 1)
                for t in range(STEPS):
                    if t < QUADS:
                        dve.wait_ge(s_score, t + 1)
                        n = t % NS
                        link(dve.tensor_reduce(negmax[:, n, :], sc_bank[t % 2][:].rearrange("p (j k) -> p j k", j=4),
                                               AX.X, ALU.max, negate=True))
                        dve.tensor_scalar(negmax[:, n, :], negmax[:, n, :], DK ** -0.5, None, ALU.mult).then_inc(s_max, 1)
                    if 2 <= t < QUADS + 2:
                        u = t - 2
                        dve.wait_ge(s_pt, u + 1)
                        if u // 2 >= 2:
                            dve.wait_ge(s_pv, u // 2 - 1)
                        dve.tensor_copy(probT[u // 2 % 2][:, 4 * (u % 2):4 * (u % 2) + 4, :].rearrange("p a b -> p (a b)"),
                                        pt_bank[u % 2][:]).then_inc(s_ptc, 1)
                    if half_in_ev(t) is not None:
                        h = half_in_ev(t)
                        b, part = h // 2, slice(4 * (h % 2), 4 * (h % 2) + 4)
                        dve.wait_ge(s_ohi, h + 1)
                        dve.tensor_tensor(oT_lo[b % 2][:, part, :].rearrange("p a b -> p (a b)"), pv_bank[h % 2][:],
                                          oT_hi[b % 2][:, part, :].rearrange("p a b -> p (a b)").bitcast(F32),
                                          ALU.subtract).then_inc(s_olo, 1)
                    done = chunk_in_o(t - 1)
                    if done and done[2] == KC - 1:
                        b, half, _ = done
                        cols = slice(half * HALF, (half + 1) * HALF)
                        dve.wait_ge(s_o, 2 * b + half + 1)
                        if half == 0:
                            dve.wait_ge(s_xb[b % 2], 16 * (b // 2 + 1))
                            if b >= 2:
                                dve.wait_ge(s_x2st[b % 2], 16 * (b // 2))
                        ins = dve.scalar_tensor_tensor(out=x2[b % 2][:, cols], in0=o_bank[half][:], scalar=gates[:, 0:1],
                                                       in1=xb[b % 2][:, cols], op0=ALU.mult, op1=ALU.add)
                        ins.then_inc(s_x2, 1)
                        dve.wait_ge(s_x2, 2 * b + half + 1)
                        dve.bn_stats(ln2_stats[:, b, half, :], x2[b % 2][:, cols])
                    if 1 <= t < QUADS + 1:
                        n = (t - 1) % NS
                        dve.wait_ge(s_exp, t)
                        dve.reciprocal(rec[:, n, :], total[:, n, :]).then_inc(s_rec, 1)

            @block.gpsimd
            def _(pool):
                for t in range(QUADS):
                    pool.wait_ge(s_rec, t + 1)
                    pool.tensor_tensor(prob[t % NP][:], prob[t % NP][:],
                                       rec[:, t % NS, :].unsqueeze(2).to_broadcast([P, 4, P]), ALU.mult).then_inc(s_norm, 1)

        with ExitStack() as st, nc.Block() as block:
            wg_hi, wg_lo = (sb(n, [P, KC, D], F32R, st) for n in ("wg_hi", "wg_lo"))
            dn_hi, dn_lo = (sb(n, [P, KC, NE * R], F32R, st) for n in ("dn_hi", "dn_lo"))
            up_hi, up_lo = (sb(n, [P, LC, D], F32R, st) for n in ("up_hi", "up_lo"))
            yT_hi = sb("yT_hi", [P, GB, KC, P], F32R, st)
            yT_lo = sb("yT_lo", [P, GB, KC, P], F32R, st)
            h_hi = sb("h_hi", [P, LC, GT], F32R, st)
            h_lo = sb("h_lo", [P, LC, GT], F32R, st)
            NX = 5
            raw = [sb(f"raw_d{i}", [P, D], F32, st) for i in range(2)]
            xm = [sb(f"xm{i}", [P, D], F32, st) for i in range(NX - 1)] + [raw[0]]
            yn = raw[1]
            wkT = sb("wkT", [P, KC, NK], F32, st)
            keysT = sb("keysT", [NK, NE], F32, st)
            mv = sb("mv_d", [P, NB, 2], F32, st)
            root = sb("root_d", [P, NB], F32, st)
            rstd = sb("rstd_d", [P, NB], F32, st)
            tmp = sb("tmp_d", [P, NB], F32, st)
            msum = sb("msum", [P, KC, GB], F32, st)
            query = sb("query", [NK, GB], F32, st)
            score = sb("score", [GB, NE], F32, st)
            smax = sb("smax", [GB, 1], F32, st)
            expo = sb("expo", [GB, NE], F32, st)
            ssum = sb("ssum", [GB, 1], F32, st)
            coef = sb("coef", [GB, NE], F32, st)
            coefw = yn[0:GB, 0:NE * R].rearrange("b (e r) -> b e r", e=NE)
            coefc = sb("coefc", [P, LC, GB], F32, st)
            s_raw = [sem(f"s_raw_d{i}") for i in range(2)]
            s_xm = [sem(f"s_xm{i}") for i in range(NX)]
            s_ost = [sem(f"s_ost{i}") for i in range(NX)]
            s_statd, s_rootd, s_yn, s_small, s_smalle = (sem(n) for n in ("s_statd", "s_rootd", "s_yn", "s_small", "s_smalle"))
            line, plan = new_line("d"), []
            raw_uses, last_raw_user = [0], {}
            t_end, out_end = {}, {}

            def raw_job(src, hi, lo, pe_fn=None, cols=D, rows=P, act=None, dve=None):
                use = raw_uses[0]
                raw_uses[0] += 1
                slot = use % 2
                free = last_raw_user.get(slot, 0)

                def load(sp):
                    if free:
                        sp.wait_ge(line.emptied, free)
                    dst = raw[slot][0:rows, 0:cols]
                    if len(src.shape) == 3:
                        dst = dst.rearrange("p (e r) -> p e r", e=src.shape[1])
                    sp.dma_start(dst, src).then_inc(s_raw[slot], 16)
                plan.append((free - 0.5, load))
                landed = 16 * (use // 2 + 1)
                part = raw[slot][:, 0:cols]
                if pe_fn is None:
                    end = line.add(Job(
                        None, lambda bank: nc.vector.tensor_tensor(lo, part, hi.bitcast(F32), ALU.subtract),
                        act=lambda bank: nc.scalar.activation(hi, part, ACT.Copy),
                        act_wait=lambda act: act.wait_ge(s_raw[slot], landed),
                        dve_wait=lambda dve: dve.wait_ge(s_raw[slot], landed)))
                else:
                    end = line.add(Job(lambda bank: pe_fn(bank, raw[slot]), dve,
                                       pe_wait=lambda pe: pe.wait_ge(s_raw[slot], landed)))
                last_raw_user[slot] = end
                return end

            weight_jobs(line, w_org, wg_hi, wg_lo, raw, s_raw, plan)
            def key_pe(half):
                def fn(bank, chunk):
                    for q in range(4):
                        k = 4 * half + q
                        last = nc.tensor.transpose(bank[:, q * P:(q + 1) * P], chunk[:, k * P:(k + 1) * P], ident[:])
                    return last
                return fn
            for half in range(2):
                raw_job(w_key, None, None, key_pe(half),
                        dve=lambda bank, half=half: nc.vector.tensor_copy(
                            wkT[:, 4 * half:4 * half + 4, :].rearrange("p a b -> p (a b)"), bank[:]))
            raw_job(lora_keys, None, None,
                    lambda bank, chunk: nc.tensor.transpose(bank[:, 0:NE], chunk[0:NE, 0:NK], ident[0:NE, 0:NE]),
                    cols=NK, rows=NE, dve=lambda bank: nc.vector.tensor_copy(keysT[:], bank[:, 0:NE]))
            for k in range(KC):
                raw_job(lora_down[:, k * P:(k + 1) * P, :].rearrange("e p r -> p e r"), dn_hi[:, k, :], dn_lo[:, k, :],
                        cols=NE * R)
            up_rows = lora_up.rearrange("e r o -> (e r) o")
            for k in range(LC):
                weights_end = raw_job(up_rows[k * P:(k + 1) * P, :], up_hi[:, k, :], up_lo[:, k, :])

            def load_xm(b):
                slot = b % NX
                free = out_end[b - NX] if b >= NX else 0

                def load(sp):
                    if free:
                        sp.wait_ge(s_ost[slot], 16 * (b // NX))
                    if b == NX - 1:
                        sp.wait_ge(line.emptied, weights_end)
                    sp.dma_start(xm[slot][:], x_mid[b * P:(b + 1) * P, :]).then_inc(s_xm[slot], 16)
                plan.append((free + 0.8 if free else weights_end + 0.1 if b == NX - 1 else 0.1 + b, load))

            def all_stats(dve):
                for b in range(NB):
                    last = dve.bn_aggr(mv[:, b, :], ln2_stats[:, b, :, :])
                link(last)
                link(dve.tensor_scalar(mv[:, :, 1:2], mv[:, :, 1:2], EPS, None, ALU.add))
                dve.sem_inc(s_statd, 1)

            def all_roots(act):
                act.wait_ge(s_statd, 1)
                act.activation(root[:], mv[:, :, 1:2].rearrange("p a b -> p (a b)"), ACT.Sqrt).then_inc(s_rootd, 1)

            def all_inverse(dve):
                dve.wait_ge(s_rootd, 1)
                inverse_root(dve, mv[:, :, 1:2].rearrange("p a b -> p (a b)"), root[:], rstd[:], tmp[:])

            line.jobs[0].dve_pre, line.jobs[0].act_pre, line.jobs[1].dve_pre = all_stats, None, all_inverse
            line.jobs[1].act_pre = all_roots

            def t_jobs(b):
                g, i = b // GB, b % GB
                load_xm(b)

                def normalise(dve):
                    dve.wait_ge(s_xm[b % NX], 16 * (b // NX + 1))
                    if b:
                        line.wait_filled(dve, t_end[b - 1])
                    else:
                        dve.wait_ge(line.emptied, weights_end)
                    dve.tensor_scalar(yn[:], xm[b % NX][:], mv[:, b, 0:1], rstd[:, b:b + 1],
                                      ALU.subtract, ALU.mult).then_inc(s_yn, 1)
                for half in range(2):
                    def pe_fn(bank, half=half):
                        for q in range(4):
                            k = 4 * half + q
                            last = nc.tensor.transpose(bank[:, q * P:(q + 1) * P], yn[:, k * P:(k + 1) * P], ident[:])
                        return last
                    part = slice(4 * half, 4 * half + 4)
                    hi = yT_hi[:, i, part, :].rearrange("p a b -> p (a b)")
                    lo = yT_lo[:, i, part, :].rearrange("p a b -> p (a b)")

                    def empty(bank, part=part, hi=hi, lo=lo):
                        nc.vector.tensor_reduce(msum[:, part, i:i + 1], bank[:].rearrange("p (q s) -> p q s", q=4),
                                                AX.X, ALU.add)
                        return split_lo(lo, bank[:], hi)
                    t_end[b] = line.add(Job(
                        pe_fn, empty, act=lambda bank, hi=hi: split_hi(hi, bank[:]),
                        pe_wait=lambda pe: pe.wait_ge(s_yn, b + 1),
                        dve_pre=normalise if half == 0 else None))

            def small_job(pe_fn, dve_fn, reads=0, act=None):
                return line.add(Job(pe_fn, dve_fn, act=act, reads=reads))

            def expert_jobs(g):
                def query_pe(bank):
                    for k in range(KC):
                        last = nc.tensor.matmul(bank[:, 0:GB], wkT[:, k, :], msum[:, k, :], start=(k == 0), stop=(k == KC - 1))
                    return last
                a = small_job(query_pe, lambda bank: nc.vector.tensor_copy(query[:], bank[:, 0:GB]),
                              reads=max(t_end[g * GB + GB - 1], weights_end))

                def score_dve(bank):
                    link(nc.vector.tensor_reduce(smax[:], bank[0:GB, 0:NE], AX.X, ALU.max, negate=True))
                    link(nc.vector.tensor_scalar(score[:], bank[0:GB, 0:NE], smax[:, 0:1], None, ALU.add))
                    nc.vector.sem_inc(s_small, 1)
                    nc.vector.wait_ge(s_smalle, g + 1)
                    link(nc.vector.reciprocal(ssum[:], ssum[:]))
                    link(nc.vector.tensor_scalar(coef[:], expo[:], ssum[:, 0:1], None, ALU.mult))
                    return nc.vector.tensor_copy(coefw, coef[:].unsqueeze(2).to_broadcast([GB, NE, R]))
                b = small_job(lambda bank: nc.tensor.matmul(bank[0:GB, 0:NE], query[:], keysT[:], start=True, stop=True),
                              score_dve, reads=a)
                line.jobs[b - 1].act_pre = lambda act: (
                    act.wait_ge(s_small, g + 1),
                    act.activation(expo[:], score[:], ACT.Exp, scale=1.0 / (S * NK ** 0.5), accum_out=ssum[:, 0:1])
                    .then_inc(s_smalle, 1))

                def spread_pe(bank):
                    flat = yn[0:GB, 0:NE * R]
                    for c in range(LC):
                        last = nc.tensor.matmul(bank[:, c * GB:(c + 1) * GB], flat[:, c * P:(c + 1) * P],
                                                ident[0:GB, 0:GB], start=True, stop=True)
                    return last
                small_job(spread_pe, lambda bank: nc.vector.tensor_copy(coefc[:].rearrange("p c b -> p (c b)"),
                                                                        bank[:, 0:LC * GB]), reads=b)
                return len(line.jobs)

            def h_job(g, c, coef_end):
                def pe_fn(bank):
                    return three_products(
                        bank[:], lambda k: (dn_hi[:, k, c * P:(c + 1) * P], dn_lo[:, k, c * P:(c + 1) * P]),
                        lambda k: (yT_hi[:, :, k, :], yT_lo[:, :, k, :]), range(KC))

                def hi_fn(bank):
                    for i in range(GB):
                        tok = slice(i * P, (i + 1) * P)
                        last = nc.scalar.activation(h_hi[:, c, tok], bank[:, tok], ACT.Copy, scale=coefc[:, c, i:i + 1])
                    return last

                def lo_fn(bank):
                    for i in range(GB):
                        tok = slice(i * P, (i + 1) * P)
                        last = nc.vector.scalar_tensor_tensor(
                            out=h_lo[:, c, tok], in0=bank[:, tok], scalar=coefc[:, c, i:i + 1],
                            in1=h_hi[:, c, tok].bitcast(F32), op0=ALU.mult, op1=ALU.subtract)
                    return last
                return line.add(Job(pe_fn, lo_fn, act=hi_fn, reads=t_end[g * GB + GB - 1],
                                    act_wait=lambda act: act.wait_ge(line.emptied, coef_end)))

            def out_job(b, half, h_end):
                i, cols = b % GB, slice(half * HALF, (half + 1) * HALF)

                def pe_fn(bank):
                    tok = slice(i * P, (i + 1) * P)
                    return three_products(
                        bank[:],
                        lambda k: (yT_hi[:, i, k, :], yT_lo[:, i, k, :]) if k < KC
                        else (h_hi[:, k - KC, tok], h_lo[:, k - KC, tok]),
                        lambda k: (wg_hi[:, k, cols], wg_lo[:, k, cols]) if k < KC
                        else (up_hi[:, k - KC, cols], up_lo[:, k - KC, cols]),
                        range(KC + LC))
                part = xm[b % NX][:, cols]
                out_end[b] = line.add(Job(
                    pe_fn, lambda bank: nc.vector.scalar_tensor_tensor(
                        out=part, in0=bank[:], scalar=gates[:, 1:2], in1=part, op0=ALU.mult, op1=ALU.add),
                    reads=max(h_end, weights_end)))

            def store_out(b):
                end = out_end[b]

                def store(sp):
                    sp.wait_ge(line.emptied, end)
                    sp.dma_start(out_t[b * P:(b + 1) * P, :], xm[b % NX][:]).then_inc(s_ost[b % NX], 16)
                plan.append((end + 0.6, store))

            for b in range(GB):
                t_jobs(b)
            for g in range(NG):
                coef_end = expert_jobs(g)
                for c in range(LC):
                    h_end = h_job(g, c, coef_end)
                for b in range(g * GB, (g + 1) * GB):
                    out_job(b, 0, h_end)
                    out_job(b, 1, h_end)
                    store_out(b)
                    if g + 1 < NG:
                        t_jobs(b + GB)

            def stores_end(sp):
                for i in range(NX):
                    sp.wait_ge(s_ost[i], 16 * len(range(i, NB, NX)))
            run_phase(block, line, plan, stores_end)


_INS = ['x', 'ctx_4096', 'g_xattn', 'g_ffn', 'L0_xattn_Wq', 'L0_xattn_bq', 'L0_xattn_Wk', 'L0_xattn_bk',
        'L0_xattn_Wv', 'L0_xattn_bv', 'L0_xattn_interference', 'L0_xattn_amp', 'L0_xattn_Wo', 'L0_xattn_bo',
        'L0_ffn_W_org', 'L0_ffn_lora_down', 'L0_ffn_lora_up', 'L0_ffn_lora_keys', 'L0_ffn_Wq']


def kernel(**inputs):
    import numpy as np
    import concourse.bacc as bacc
    from concourse.bass_utils import run_bass_kernel_spmd

    nc = bacc.Bacc("TRN2", target_bir_lowering=False, num_devices=1)
    arrays, args = {}, []
    for name in _INS:
        a = np.ascontiguousarray(inputs[name])
        arrays[f"in_{name}"] = a
        args.append(nc.dram_tensor(f"in_{name}", a.shape, mybir.dt.from_np(a.dtype), kind="ExternalInput").ap())
    args.append(nc.dram_tensor("out_x", inputs['x'].shape, F32, kind="ExternalOutput").ap())
    build(nc, *args)
    r = run_bass_kernel_spmd(nc, [arrays], core_ids=[0])
    return r.results[0]["out_x"]
```

```python
from contextlib import ExitStack

import concourse.bass as bass
from concourse import mybir

F32 = mybir.dt.float32
F32R = mybir.dt.float32r
ALU = mybir.AluOpType
ACT = mybir.ActivationFunctionType
AX = mybir.AxisListType

P = 128
EPS = 1e-5


class Job:

    def __init__(self, pe, dve, act=None, reads=0, pe_wait=None, act_wait=None, dve_wait=None,
                 act_pre=None, dve_pre=None):
        self.pe, self.dve, self.act, self.reads = pe, dve, act, reads
        self.pe_wait, self.act_wait, self.dve_wait = pe_wait, act_wait, dve_wait
        self.act_pre, self.dve_pre = act_pre, dve_pre


class Line:

    def __init__(self, banks, filled, scaled, emptied):
        self.banks, self.jobs = banks, []
        self.filled, self.scaled, self.emptied = filled, scaled, emptied

    def add(self, job):
        self.jobs.append(job)
        return len(self.jobs)

    def bank(self, n):
        return self.banks[n % len(self.banks)]

    def wait_filled(self, eng, end):
        eng.wait_ge(self.filled, sum(1 for job in self.jobs[:end] if job.pe))

    def run_tensor(self, pe):
        ring = len(self.banks)
        for n, job in enumerate(self.jobs):
            need = max(n + 1 - ring, job.reads, 0)
            if job.pe:
                if need:
                    pe.wait_ge(self.emptied, need)
                if job.pe_wait:
                    job.pe_wait(pe)
                job.pe(self.bank(n)).then_inc(self.filled, 1)

    def run_scalar(self, act):
        for n, job in enumerate(self.jobs):
            if job.act_pre:
                job.act_pre(act)
            if job.act:
                if job.pe:
                    self.wait_filled(act, n + 1)
                if job.act_wait:
                    job.act_wait(act)
                job.act(self.bank(n)).then_inc(self.scaled, 1)

    def run_vector(self, dve):
        scaled = 0
        for n, job in enumerate(self.jobs):
            if job.dve_pre:
                job.dve_pre(dve)
            if job.act:
                scaled += 1
                dve.wait_ge(self.scaled, scaled)
            else:
                self.wait_filled(dve, n + 1)
            if job.dve_wait:
                job.dve_wait(dve)
            job.dve(self.bank(n)).then_inc(self.emptied, 1)


def build(nc, x, ctx_in, g_xattn, g_ffn, wq, bq, wk, bk, wv, bv, interference, amp, wo, bo,
          w_org, lora_down, lora_up, lora_keys, w_key, out):
    NB, S, D = x.shape
    NH, NM, _ = interference.shape
    DK = D // (NH * NM)
    HM = NH * NM
    NE, _, R = lora_down.shape
    NK = w_key.shape[0]
    T = NB * S
    KC = D // P
    GB = 4
    NG = NB // GB
    GT = GB * S
    HALF = 512
    LC = NE * R // P
    STACK = 3 * DK
    OCT = P // DK
    NOCT = HM // OCT
    PAIRS = HM // 2
    assert S == P and OCT == 8 and T % GT == 0

    x_t = x.rearrange("b s d -> (b s) d")
    ctx_t = ctx_in.rearrange("b s d -> (b s) d")
    out_t = out.rearrange("b s d -> (b s) d")

    k_stack = nc.dram_tensor("k_stack", (HM, 3, DK, T), F32, kind="Internal").ap()
    q_stack = nc.dram_tensor("q_stack", (HM, 3, DK, T), F32, kind="Internal").ap()
    v_pad = nc.dram_tensor("v_pad", (T, PAIRS * 2 * 32), F32, kind="Internal").ap()
    x_mid = nc.dram_tensor("x_mid", (T, D), F32, kind="Internal").ap()

    top = ExitStack()
    with top:
        def sem(name):
            return top.enter_context(nc.semaphore(name))

        def sb(name, shape, dt=F32, stack=top):
            return stack.enter_context(nc.sbuf_tensor(name, shape, dt))

        banks = [top.enter_context(nc.psum_tensor(f"bank{i}", [P, HALF], F32)) for i in range(8)]

        ident = sb("ident", [P, P])
        ln2_stats = sb("ln2_stats", [P, NB, 2, 6])
        gates = sb("gates", [P, 2])
        s_const = sem("s_const")
        s_chain = sem("s_chain")
        chain = [0]

        def link(ins):
            chain[0] += 1
            ins.then_inc(s_chain, 1)
            nc.vector.wait_ge(s_chain, chain[0])

        def split_hi(hi, bank_ap, **kw):
            return nc.scalar.activation(hi, bank_ap, ACT.Copy, **kw)

        def split_lo(lo, bank_ap, hi):
            return nc.vector.tensor_tensor(lo, bank_ap, hi.bitcast(F32), ALU.subtract)

        def three_products(bank_ap, station, moving, chunks):
            last = None
            for i, k in enumerate(chunks):
                (sh, sl), (mh, ml) = station(k), moving(k)
                nc.tensor.matmul(bank_ap, sh, mh, start=(i == 0), stop=False)
                nc.tensor.matmul(bank_ap, sh, ml, start=False, stop=False)
                last = nc.tensor.matmul(bank_ap, sl, mh, start=False, stop=(i == len(chunks) - 1))
            return last

        w1_hi, w1_lo = (sb(n, [P, KC, D], F32R) for n in ("w1_hi", "w1_lo"))

        proj = ExitStack()
        w0_hi, w0_lo = (sb(n, [P, KC, D], F32R, proj) for n in ("w0_hi", "w0_lo"))
        mix = sb("mix", [P, KC, P], stack=proj)
        bias_mixed = sb("bias_mixed", [P, 2, KC], stack=proj)
        bv_row = sb("bv_row", [P, D], stack=proj)
        NRAW = 3
        raw = [sb(f"raw{i}", [P, D], F32, proj) for i in range(NRAW)]
        tin = [sb(f"tin{i}", [P, D], F32, proj) for i in range(2)]
        s_raw = [sem(f"s_raw{i}") for i in range(NRAW)]
        s_tin = [sem(f"s_tin{i}") for i in range(2)]

        with ExitStack() as st, nc.Block() as block:
            jm = sb("jm", [NM, NH, NM], stack=st)
            amp4 = sb("amp4", [NM, 1], stack=st)
            braw = sb("braw", [3 * KC, P], stack=st)
            graw = sb("graw", [P, 2], stack=st)
            rowsel = sb("rowsel", [NM, P // NM, NM], stack=st)
            jrow = sb("jrow", [P, NH, NM], stack=st)
            group = sb("group", [P, P // NM], stack=st)
            bcol = sb("bcol", [P, 3 * KC], stack=st)
            bvb = sb("bvb", [P, KC, P], stack=st)
            s_in, s_id, s_ready, s_mm, s_g = (sem(n) for n in ("s_in", "s_id", "s_ready", "s_mm", "s_g"))

            @block.sync
            def _(sp):
                sp.dma_start(raw[0][:], wk[0:P, :]).then_inc(s_raw[0], 16)
                with nc.allow_non_contiguous_dma(reason="a few hundred small elements"):
                    sp.dma_start(jm[:], interference.rearrange("h i j -> i h j")).then_inc(s_in, 16)
                    sp.dma_start(amp4[:], amp.partition_broadcast(NM)).then_inc(s_in, 16)
                    sp.dma_start(graw[:, 0:1], g_xattn.partition_broadcast(P)).then_inc(s_in, 16)
                    sp.dma_start(graw[:, 1:2], g_ffn.partition_broadcast(P)).then_inc(s_in, 16)
                    for i, b in enumerate((bk, bq, bv)):
                        sp.dma_start(braw[i * KC:(i + 1) * KC, :],
                                     b.rearrange("(c i) -> c i", i=P)).then_inc(s_in, 16)
                for i in range(1, NRAW):
                    sp.dma_start(raw[i][:], wk[i * P:(i + 1) * P, :]).then_inc(s_raw[i], 16)
                for i in range(2):
                    sp.dma_start(tin[i][:], ctx_t[i * P:(i + 1) * P, :]).then_inc(s_tin[i], 16)

            @block.gpsimd
            def _(pool):
                pool.memset(ident[:], 0.0).then_inc(s_id, 1)
                pool.wait_ge(s_id, 1)
                pool.affine_select(out=ident[:], in_=ident[:], compare_op=ALU.not_equal, fill=1.0, base=0,
                                   pattern=[[-1, P]], channel_multiplier=1).then_inc(s_id, 1)

            @block.scalar
            def _(act):
                act.wait_ge(s_in, 7 * 16)
                act.activation(gates[:], graw[:], ACT.Tanh).then_inc(s_g, 1)

            @block.vector
            def _(dve):
                dve.wait_ge(s_in, 7 * 16)
                dve.wait_ge(s_id, 2)
                dve.tensor_copy(rowsel[:], ident[0:NM, 0:NM].unsqueeze(1).to_broadcast([NM, P // NM, NM]))
                dve.tensor_reduce(group[:], ident[:].rearrange("p (g f) -> p g f", f=NM), AX.X, ALU.add)
                link(dve.tensor_scalar(jm[:], jm[:], amp4[:, 0:1], 0.1, ALU.mult, ALU.mult))
                link(dve.tensor_tensor(jm[:], jm[:],
                                       ident[0:NM, 0:NM].unsqueeze(1).to_broadcast([NM, NH, NM]), ALU.add))
                dve.sem_inc(s_ready, 1)
                dve.wait_ge(s_mm, 2)
                dve.tensor_copy(jrow[:].rearrange("p h m -> p (h m)"), banks[0][:, 0:HM])
                link(dve.tensor_copy(bcol[:], banks[1][:, 0:3 * KC]))
                for c in range(KC):
                    for h2 in range(2):
                        width = P // 2
                        dst = mix[:, c, h2 * width:(h2 + 1) * width].rearrange("p (m d) -> p m d", m=NM)
                        dve.tensor_tensor(
                            dst, jrow[:, 2 * c + h2, :].unsqueeze(2).to_broadcast([P, NM, DK]),
                            group[:, h2 * DK:(h2 + 1) * DK].unsqueeze(1).to_broadcast([P, NM, DK]), ALU.mult)
                link(dve.tensor_copy(bvb[:], bcol[:, 2 * KC:3 * KC].unsqueeze(2).to_broadcast([P, KC, P])))
                dve.sem_inc(s_ready, 1)
                dve.wait_ge(s_mm, 3)
                dve.tensor_copy(bias_mixed[:, 0, :], banks[2][:, 0:KC])
                dve.tensor_scalar(bias_mixed[:, 1, :], banks[2][:, KC:2 * KC], DK ** -0.5, None, ALU.mult)
                dve.tensor_copy(bv_row[:, 0:HALF], banks[3][:])
                link(dve.tensor_copy(bv_row[:, HALF:D], banks[4][:]))

            @block.tensor
            def _(pe):
                pe.wait_ge(s_ready, 1)
                pe.wait_ge(s_in, 7 * 16)
                pe.matmul(banks[0][:, 0:HM], rowsel[:].rearrange("m g f -> m (g f)"),
                          jm[:].rearrange("i h j -> i (h j)"), start=True, stop=True).then_inc(s_mm, 1)
                pe.transpose(banks[1][:, 0:3 * KC], braw[:], ident[0:3 * KC, 0:3 * KC]).then_inc(s_mm, 1)
                pe.wait_ge(s_ready, 2)
                for a in range(2):
                    for c in range(KC):
                        pe.matmul(banks[2][:, a * KC + c:a * KC + c + 1], mix[:, c, :],
                                  bcol[:, a * KC + c:a * KC + c + 1], start=True, stop=True)
                for c in range(KC):
                    last = pe.matmul(banks[3 + c // 4][:, (c % 4) * P:(c % 4 + 1) * P], bvb[:, c, :],
                                     mix[:, c, :], start=True, stop=True)
                last.then_inc(s_mm, 1)

        class RawRing:

            def __init__(self, line, plan, tiles, sems, preloaded=0):
                self.line, self.plan, self.tiles, self.sems = line, plan, tiles, sems
                self.uses, self.last, self.preloaded = 0, {}, preloaded

            def take(self, src, ahead=0.5):
                slot, n = self.uses % len(self.tiles), self.uses // len(self.tiles) + 1
                free = self.last.get(slot, 0)

                def load(sp):
                    if free:
                        sp.wait_ge(self.line.emptied, free)
                    dst = self.tiles[slot][0:src.shape[0], 0:src.shape[-1]]
                    sp.dma_start(dst, src).then_inc(self.sems[slot], 16)

                if self.uses >= self.preloaded:
                    self.plan.append((free - ahead, load))
                self.uses += 1
                return slot, lambda eng: eng.wait_ge(self.sems[slot], 16 * n)

            def release(self, slot, end):
                self.last[slot] = end

        def weight_chunk(line, ring, w, c, w_hi, w_lo, mixed=None, reorder=None, reads=0):
            slot, landed = ring.take(w[c * P:(c + 1) * P, :])

            def reorder_inputs(dve):
                tiles, done, first = reorder
                tile = tiles[c % len(tiles)]
                landed(dve)
                if c >= len(tiles):
                    line.wait_filled(dve, first + 2 * (c - len(tiles)) + 2)
                for m in range(NM):
                    last = dve.tensor_copy(tile[:].rearrange("p (h m d) -> p h m d", h=NH, m=NM)[:, :, m, :],
                                           ring.tiles[slot][:].rearrange("p (h d m) -> p h m d", h=NH, m=NM)[:, :, m, :])
                last.then_inc(done, 1)

            for half in range(2):
                def pe_fn(bank, half=half):
                    src = reorder[0][c % len(reorder[0])] if reorder else ring.tiles[slot]
                    for q in range(4):
                        rows = src[:, (4 * half + q) * P:(4 * half + q + 1) * P]
                        dst = bank[:, q * P:(q + 1) * P]
                        if mixed is not None:
                            last = nc.tensor.matmul(dst, rows, mixed[:, c, :], start=True, stop=True)
                        else:
                            last = nc.tensor.transpose(dst, rows, ident[:])
                    return last

                hi = w_hi[:, 4 * half:4 * half + 4, c * P:(c + 1) * P]
                lo = w_lo[:, 4 * half:4 * half + 4, c * P:(c + 1) * P]
                end = line.add(Job(
                    pe_fn, lambda bank, hi=hi, lo=lo: split_lo(lo, bank[:].rearrange("p (q r) -> p q r", q=4), hi),
                    act=lambda bank, hi=hi: split_hi(hi, bank[:].rearrange("p (q r) -> p q r", q=4)),
                    pe_wait=(lambda pe: pe.wait_ge(reorder[1], c + 1)) if reorder else landed, reads=reads))
            ring.release(slot, end)
            return end, reorder_inputs

        def transpose_jobs(line, tile, wait, hi, lo, sums=None, dve_pre=None):
            for half in range(2):
                def pe_fn(bank, half=half):
                    for q in range(4):
                        k = 4 * half + q
                        last = nc.tensor.transpose(bank[:, q * P:(q + 1) * P], tile[:, k * P:(k + 1) * P], ident[:])
                    return last

                part = slice(4 * half, 4 * half + 4)
                flat_hi = hi[:, part, :].rearrange("p a b -> p (a b)")
                flat_lo = lo[:, part, :].rearrange("p a b -> p (a b)")

                def empty(bank, part=part, flat_hi=flat_hi, flat_lo=flat_lo):
                    if sums is not None:
                        nc.vector.tensor_reduce(sums[:, part, :], bank[:].rearrange("p (q s) -> p q s", q=4),
                                                AX.X, ALU.add)
                    return split_lo(flat_lo, bank[:], flat_hi)
                end = line.add(Job(pe_fn, empty, act=lambda bank, flat_hi=flat_hi: split_hi(flat_hi, bank[:]),
                                   pe_wait=wait, dve_pre=dve_pre if half == 0 else None))
            return end

        def inverse_root(dve, var, root, rstd, tmp):
            link(dve.reciprocal(rstd, root))
            link(dve.tensor_tensor(tmp, rstd, rstd, ALU.mult))
            link(dve.tensor_tensor(tmp, tmp, var, ALU.mult))
            link(dve.tensor_scalar(tmp, tmp, -0.5, 1.5, ALU.mult, ALU.add))
            link(dve.tensor_tensor(rstd, rstd, tmp, ALU.mult))

        def run_phase(block, line, plan, stores_end=None):
            @block.sync
            def _(sp):
                for _, step in sorted(plan, key=lambda e: e[0]):
                    step(sp)
                if stores_end:
                    stores_end(sp)

            @block.tensor
            def _(pe):
                line.run_tensor(pe)

            @block.scalar
            def _(act):
                line.run_scalar(act)

            @block.vector
            def _(dve):
                line.run_vector(dve)

        def new_line(tag):
            return Line(banks, sem(f"s_filled_{tag}"), sem(f"s_scaled_{tag}"), sem(f"s_emptied_{tag}"))

        def stacked(scratch, c, section, g):
            return scratch[c * OCT:(c + 1) * OCT, section, :, g * GT:(g + 1) * GT]

        def projection_store(line, plan, scratch, hi, lo, s_free, c, g, end, hi_sections, lo_section):
            def store(sp):
                sp.wait_ge(line.emptied, end)
                for section in range(3):
                    src = lo if section == lo_section else hi
                    sp.dma_start(stacked(scratch, c, section, g), src[:].bitcast(F32)).then_inc(s_free, 16)
            plan.append((end + 0.6, store))

        with proj, ExitStack() as st, nc.Block() as block:
            cT_hi = sb("cT_hi", [P, GB, KC, P], F32R, st)
            cT_lo = sb("cT_lo", [P, GB, KC, P], F32R, st)
            stage_hi = [sb(f"stage_hi{i}", [P, GT], F32R, st) for i in range(2)]
            stage_lo = [sb(f"stage_lo{i}", [P, GT], F32R, st) for i in range(2)]
            v_out = [sb(f"v_out{i}", [P, PAIRS // 2, 2, 32], F32, st) for i in range(2)]
            reordered = [v[:].rearrange("p q a d -> p (q a d)") for v in v_out]
            stats = sb("stats", [P, 2, 6], F32, st)
            mv = sb("mv", [P, 2], F32, st)
            root = sb("root", [P, 1], F32, st)
            rstd = sb("rstd", [P, 1], F32, st)
            tmp = sb("tmp", [P, 1], F32, st)
            s_stage = [sem(f"s_stage{i}") for i in range(2)]
            s_vst = [sem(f"s_vst{i}") for i in range(2)]
            s_stat, s_root, s_xn, s_reordered = (sem(n) for n in ("s_stat", "s_root", "s_xn", "s_reordered"))
            line, plan = new_line("a"), []
            ring = RawRing(line, plan, raw, s_raw, preloaded=NRAW)

            odd_hi = w1_hi[:, 0:KC // 2, :].rearrange("p a (b c) -> p (a b) c", c=P).rearrange("p (i k) c -> p i k c", i=GB)
            odd_lo = w1_hi[:, KC // 2:KC, :].rearrange("p a (b c) -> p (a b) c", c=P).rearrange("p (i k) c -> p i k c", i=GB)

            def x_place(g):
                return (cT_hi[:], cT_lo[:]) if g % 2 == 0 else (odd_hi, odd_lo)

            t_end = {}

            def load_input(n):
                slot, free = n % 2, t_end.get(n - 2, 0)
                src = ctx_t[n * P:(n + 1) * P, :] if n < NB else x_t[(n - NB) * P:(n - NB + 1) * P, :]

                def load(sp):
                    line.wait_filled(sp, free)
                    sp.dma_start(tin[slot][:], src).then_inc(s_tin[slot], 16)
                if n >= 2:
                    plan.append((free - 0.5, load))

            def ctx_jobs(b):
                load_input(b)
                t_end[b] = transpose_jobs(
                    line, tin[b % 2], lambda pe: pe.wait_ge(s_tin[b % 2], 16 * (b // 2 + 1)),
                    cT_hi[:, b % GB, :, :], cT_lo[:, b % GB, :, :])

            def x_stats(b):
                n = NB + b

                def pre(dve):
                    if b:
                        dve.wait_ge(s_xn, b)
                    dve.wait_ge(s_tin[n % 2], 16 * (n // 2 + 1))
                    for h in range(2):
                        last = dve.bn_stats(stats[:, h, :], tin[n % 2][:, h * HALF:(h + 1) * HALF])
                    link(last)
                    link(dve.bn_aggr(mv[:], stats[:]))
                    dve.tensor_scalar(mv[:, 1:2], mv[:, 1:2], EPS, None, ALU.add).then_inc(s_stat, 1)
                return pre

            def x_root(b):
                def pre(act):
                    act.wait_ge(s_stat, b + 1)
                    act.activation(root[:], mv[:, 1:2], ACT.Sqrt).then_inc(s_root, 1)
                return pre

            def x_normalise(b):
                n = NB + b

                def pre(dve):
                    dve.wait_ge(s_root, b + 1)
                    inverse_root(dve, mv[:, 1:2], root[:], rstd[:], tmp[:])
                    dve.tensor_scalar(tin[n % 2][:], tin[n % 2][:], mv[:, 0:1], rstd[:, 0:1],
                                      ALU.subtract, ALU.mult).then_inc(s_xn, 1)
                return pre

            def x_jobs(b):
                g = b // GB
                hi, lo = x_place(g)
                t_end[NB + b] = transpose_jobs(line, tin[b % 2], lambda pe: pe.wait_ge(s_xn, b + 1),
                                               hi[:, b % GB, :, :], lo[:, b % GB, :, :])

            staged = [0]

            def projection_job(weight_end, input_end, hi_in, lo_in, bias, scratch, c, g, lo_section):
                slot, use = staged[0] % 2, staged[0] // 2
                staged[0] += 1
                hi, lo = stage_hi[slot], stage_lo[slot]

                def pe_fn(bank):
                    return three_products(
                        bank[:], lambda k: (w0_hi[:, k, c * P:(c + 1) * P], w0_lo[:, k, c * P:(c + 1) * P]),
                        lambda k: (hi_in[:, :, k, :], lo_in[:, :, k, :]), range(KC))

                def stage_free(act):
                    if use:
                        act.wait_ge(s_stage[slot], 48 * use)
                job = Job(
                    pe_fn,
                    lambda bank: nc.vector.scalar_tensor_tensor(
                        out=lo[:], in0=bank[:], scalar=bias, in1=hi[:].bitcast(F32), op0=ALU.add, op1=ALU.subtract),
                    act=lambda bank: nc.scalar.activation(hi[:], bank[:], ACT.Identity, bias=bias),
                    reads=max(input_end, weight_end), act_wait=stage_free)
                end = line.add(job)

                def store(sp):
                    sp.wait_ge(line.emptied, end)
                    for section in range(3):
                        src = lo if section == lo_section else hi
                        sp.dma_start(scratch[c * OCT:(c + 1) * OCT, section, :, g * GT:(g + 1) * GT],
                                     src[:].bitcast(F32)).then_inc(s_stage[slot], 16)
                plan.append((end + 0.6, store))
                return job

            def k_job(g, c):
                return projection_job(wk_end, t_end[g * GB + GB - 1], cT_hi[:], cT_lo[:], bias_mixed[:, 0, c:c + 1],
                                      k_stack, c, g, 2)

            def q_job(g, c):
                return projection_job(wq_end, t_end[NB + g * GB + GB - 1], *x_place(g), bias_mixed[:, 1, c:c + 1],
                                      q_stack, c, g, 1)

            def v_job(b, half):
                n = 2 * b + half
                slot, use = n % 2, n // 2
                gslot = b % GB
                cols = slice(half * HALF, (half + 1) * HALF)

                def pe_fn(bank):
                    return three_products(
                        bank[:], lambda k: (cT_hi[:, gslot, k, :], cT_lo[:, gslot, k, :]),
                        lambda k: (w1_hi[:, k, cols], w1_lo[:, k, cols]), range(KC))

                def empty(bank):
                    def by_pair(ap):
                        return ap.rearrange("p (q a d) -> p q a d", a=2, d=DK)
                    for a in range(2):
                        last = nc.vector.tensor_tensor(v_out[slot][:, :, a, a * DK:(a + 1) * DK], by_pair(bank[:])[:, :, a, :],
                                                       by_pair(bv_row[:, cols])[:, :, a, :], ALU.add)
                    return last

                def stage_free(dve):
                    if use:
                        dve.wait_ge(s_vst[slot], 16 * use)
                job = Job(pe_fn, empty, reads=max(t_end[b], wv_end), dve_wait=stage_free)
                end = line.add(job)

                def store(sp):
                    sp.wait_ge(line.emptied, end)
                    width = PAIRS * 32
                    sp.dma_start(v_pad[b * P:(b + 1) * P, half * width:(half + 1) * width],
                                 v_out[slot][:].rearrange("p q a d -> p (q a d)")).then_inc(s_vst[slot], 16)
                plan.append((end + 0.6, store))
                return job

            for c in range(KC):
                wk_end, _ = weight_chunk(line, ring, wk, c, w0_hi, w0_lo, mixed=mix)
                if c % 2:
                    ctx_jobs(c // 2)
            line.jobs[0].dve_pre = lambda dve: [link(dve.memset(v[:], 0.0)) for v in v_out]
            for c in range(KC):
                k_job(0, c)
                wv_end, _ = weight_chunk(line, ring, wv, c, w1_hi, w1_lo, mixed=mix)
            for g in range(NG):
                for b in range(g * GB, (g + 1) * GB):
                    first = v_job(b, 0)
                    if g + 1 < NG:
                        v_job(b, 1)
                        ctx_jobs(b + GB)
                        continue
                    xb = b - g * GB
                    load_input(NB + xb)
                    for c in (2 * xb, 2 * xb + 1):
                        wq_end, _ = weight_chunk(line, ring, wq, c, w0_hi, w0_lo, mixed=mix, reads=mix_scaled)
                    second = v_job(b, 1)
                    line.jobs[-4].dve_pre, line.jobs[-3].act_pre = x_stats(xb), x_root(xb)
                    second.dve_pre = x_normalise(xb)
                    x_jobs(xb)
                if g + 1 < NG:
                    for c in range(KC):
                        job = k_job(g + 1, c)
                        if g + 2 == NG and c == 0:
                            def scale_mix(dve):
                                line.wait_filled(dve, wv_end)
                                link(dve.tensor_scalar(mix[:], mix[:], DK ** -0.5, None, ALU.mult))
                            job.dve_pre, mix_scaled = scale_mix, len(line.jobs)
            for g in range(NG):
                for c in range(KC):
                    job = q_job(g, c)
                    nb = (g + 1) * GB + c // 2
                    if nb < NB and c % 2 == 0:
                        load_input(NB + nb)
                        job.dve_pre = x_stats(nb)
                    if nb < NB and c % 2:
                        job.act_pre, job.dve_pre = x_root(nb), x_normalise(nb)
                        x_jobs(nb)
            first = len(line.jobs)
            carriers = [line.jobs[-2], line.jobs[-1]]
            for c in range(KC):
                _, reorder_inputs = weight_chunk(line, ring, wo, c, w1_hi, w1_lo,
                                                 reorder=(reordered, s_reordered, first))
                carriers[c].dve_pre = reorder_inputs
                if c:
                    carriers.append(line.jobs[-2])
                if c == 0:
                    def v_stored(dve, step=reorder_inputs):
                        for i in range(2):
                            dve.wait_ge(s_vst[i], 16 * NB)
                        step(dve)
                    carriers[0].dve_pre = v_stored

            def stores_end(sp):
                for i in range(2):
                    sp.wait_ge(s_stage[i], 48 * NG * KC)
                    sp.wait_ge(s_vst[i], 16 * NB)
            run_phase(block, line, plan, stores_end)

        wo_hi, wo_lo = w1_hi, w1_lo
        dn_hi, dn_lo = (sb(n, [P, KC, NE * R], F32R) for n in ("dn_hi", "dn_lo"))
        with ExitStack() as st, nc.Block() as block:
            KQ = 4
            q_in = [sb(f"q_in{i}", [2 * STACK, 4, P], F32R, st) for i in range(KQ)]
            k_in = [sb(f"k_in{i}", [2 * STACK, 4, 2, P], F32R, st) for i in range(KQ)]
            v_in = [sb(f"v_in{i}", [P, PAIRS, 2, 32], F32, st) for i in range(2)]
            NP = 6
            prob = [sb(f"prob{i}", [P, 4, P], F32, st) for i in range(NP)]
            probT = [sb(f"probT{i}", [P, OCT, P], F32, st) for i in range(2)]
            NS = 8
            negmax = sb("negmax", [P, NS, 4], F32, st)
            total = sb("total", [P, NS, 4], F32, st)
            rec = sb("rec", [P, NS, 4], F32, st)
            oT_hi = [sb(f"oT_hi{i}", [P, NOCT, P], F32R, st) for i in range(2)]
            oT_lo = [sb(f"oT_lo{i}", [P, NOCT, P], F32R, st) for i in range(2)]
            bo_row = sb("bo_row", [P, D], F32, st)
            xb = [sb(f"xb{i}", [P, D], F32, st) for i in range(2)]
            x2 = [sb(f"x2_{i}", [P, D], F32, st) for i in range(2)]
            dn_raw = [sb(f"dn_raw{i}", [P, NE * R], F32, st) for i in range(2)]
            NSC = 3
            sc_bank, pt_bank, pv_bank, o_bank = banks[0:NSC], banks[3:5], banks[5:7], banks[7]

            s_kq = [sem(f"s_kq{i}") for i in range(KQ)]
            s_v = [sem(f"s_v{i}") for i in range(2)]
            s_xb = [sem(f"s_xb{i}") for i in range(2)]
            s_x2st = [sem(f"s_x2st{i}") for i in range(2)]
            s_dn = [sem(f"s_dn{i}") for i in range(2)]
            (s_zero, s_score, s_max, s_exp, s_rec, s_norm, s_pt, s_ptc, s_pv, s_ohi, s_olo, s_o, s_x2,
             s_bo, s_bog, s_xbo, s_dhi, s_dlo) = (
                sem(n) for n in ("s_zero", "s_score", "s_max", "s_exp", "s_rec", "s_norm", "s_pt", "s_ptc",
                                 "s_pv", "s_ohi", "s_olo", "s_o", "s_x2", "s_bo", "s_bog", "s_xbo", "s_dhi", "s_dlo"))

            QUADS = NB * HM // 4
            QB = HM // 4
            OCTS = NB * NOCT
            T_LAG, PV_LAG, EV_AT, O_AT = 4, 6, 14, 24
            STEPS = QB * (NB - 1) + O_AT + 2 * KC + 2

            def oct_in_pv(t):
                o = (t - PV_LAG) // 2
                return o if t >= PV_LAG and t % 2 == 0 and o < OCTS else None

            def half_in_ev(t):
                h = (t - EV_AT) // 8
                return h if t >= EV_AT and (t - EV_AT) % 8 == 0 and h < 2 * NB else None

            def chunk_in_o(t):
                j = t - O_AT
                return (j // QB, j % QB // KC, j % KC) if 0 <= j < QB * NB else None

            DN_OCT, DN_STEP = 16, 30

            def chunk_in_dn(t):
                n = (t - DN_STEP) // 4
                return n if t >= DN_STEP and (t - DN_STEP) % 4 == 0 and n < KC else None

            @block.sync
            def _(sp):
                sp.wait_ge(s_zero, 1)

                def load_oct(o):
                    slot, b, first = o % KQ, o // NOCT, (o % NOCT) * OCT
                    if o >= KQ:
                        sp.wait_ge(s_score, 2 * (o - KQ) + 2)
                    tok = slice(b * P, (b + 1) * P)
                    sp.dma_start(
                        q_in[slot][:].bitcast(F32),
                        q_stack[first:first + OCT, :, :, tok].rearrange("(p a) s d t -> (a s d) p t", a=2)
                    ).then_inc(s_kq[slot], 16)
                    for a in range(2):
                        sp.dma_start(
                            k_in[slot][a * STACK:(a + 1) * STACK, :, a, :].bitcast(F32),
                            k_stack[first + a:first + OCT:2, :, :, tok].rearrange("p s d t -> (s d) p t")
                        ).then_inc(s_kq[slot], 16)

                def load_v(b):
                    if b >= 2:
                        sp.wait_ge(s_pv, NOCT * (b - 1))
                    sp.dma_start(v_in[b % 2][:].rearrange("p q a d -> p (q a d)"),
                                 v_pad[b * P:(b + 1) * P, :]).then_inc(s_v[b % 2], 16)

                def store_x2(b):
                    sp.wait_ge(s_x2, 2 * b + 2)
                    sp.dma_start(x_mid[b * P:(b + 1) * P, :], x2[b % 2][:]).then_inc(s_x2st[b % 2], 16)

                def load_xb(b):
                    sp.dma_start(xb[b % 2][:], x_t[b * P:(b + 1) * P, :]).then_inc(s_xb[b % 2], 16)

                def load_dn(n):
                    if n >= 2:
                        sp.wait_ge(s_dlo, n - 1)
                    sp.dma_start(dn_raw[n % 2][:].rearrange("p (e r) -> p e r", e=NE),
                                 lora_down[:, n * P:(n + 1) * P, :].rearrange("e p r -> p e r")).then_inc(s_dn[n % 2], 16)

                for o in range(OCTS):
                    b = o // NOCT
                    load_oct(o)
                    if o == 0:
                        sp.dma_start(bo_row[:], bo.partition_broadcast(P)).then_inc(s_bo, 16)
                    if DN_OCT <= o < DN_OCT + 2 * KC and o % 2 == 0:
                        load_dn((o - DN_OCT) // 2)
                    if o % NOCT == 1:
                        load_v(b)
                    if o % NOCT == NOCT - 1:
                        if b >= 2:
                            store_x2(b - 2)
                        load_xb(b)
                store_x2(NB - 2)
                store_x2(NB - 1)
                for i in range(2):
                    sp.wait_ge(s_x2st[i], 16 * (NB // 2))

            @block.tensor
            def _(pe):
                for t in range(STEPS):
                    if t < QUADS:
                        o, slot = t // 2, t // 2 % KQ
                        if t % 2 == 0:
                            pe.wait_ge(s_kq[slot], 48 * (o // KQ + 1))
                        if t >= NSC:
                            pe.wait_ge(s_exp, t - NSC + 1)
                        for i in range(2):
                            p = 2 * (t % 2) + i
                            last = pe.matmul(sc_bank[t % NSC][:, i * 2 * P:(i + 1) * 2 * P], q_in[slot][:, p, :],
                                             k_in[slot][:, p, :, :].rearrange("r a k -> r (a k)"), start=True, stop=True)
                        last.then_inc(s_score, 1)
                    if T_LAG <= t < QUADS + T_LAG:
                        u = t - T_LAG
                        pe.wait_ge(s_norm, u + 1)
                        if u >= 2:
                            pe.wait_ge(s_ptc, u - 1)
                        for j in range(4):
                            last = pe.transpose(pt_bank[u % 2][:, j * P:(j + 1) * P], prob[u % NP][:, j, :], ident[:])
                        last.then_inc(s_pt, 1)
                    if oct_in_pv(t) is not None:
                        o = oct_in_pv(t)
                        b, h = o // NOCT, o // 4
                        pe.wait_ge(s_ptc, 2 * o + 2)
                        if o % NOCT == 0:
                            pe.wait_ge(s_v[b % 2], 16 * (b // 2 + 1))
                        if o % 4 == 0 and h >= 2:
                            pe.wait_ge(s_olo, h - 1)
                        for a in range(2):
                            for p in range(4):
                                last = pe.matmul(
                                    pv_bank[h % 2][32 * p:32 * p + 32, (o % 4) * P:(o % 4 + 1) * P],
                                    v_in[b % 2][:, 4 * (o % NOCT) + p, a, :], probT[o % 2][:, 2 * p + a, :],
                                    start=(a == 0), stop=(a == 1), skip_group_check=True)
                        last.then_inc(s_pv, 1)
                    if chunk_in_o(t):
                        b, half, k = chunk_in_o(t)
                        if k == 0:
                            pe.wait_ge(s_olo, 2 * b + 2)
                            if 2 * b + half:
                                pe.wait_ge(s_x2, 2 * b + half)
                        cols = slice(half * HALF, (half + 1) * HALF)
                        hi, lo = oT_hi[b % 2], oT_lo[b % 2]
                        pe.matmul(o_bank[:], hi[:, k, :], wo_hi[:, k, cols], start=(k == 0), stop=False)
                        pe.matmul(o_bank[:], hi[:, k, :], wo_lo[:, k, cols], start=False, stop=False)
                        last = pe.matmul(o_bank[:], lo[:, k, :], wo_hi[:, k, cols], start=False, stop=(k == KC - 1))
                        if k == KC - 1:
                            last.then_inc(s_o, 1)

            @block.scalar
            def _(act):
                for t in range(STEPS):
                    if t < QUADS:
                        act.wait_ge(s_max, t + 1)
                        if t >= NP:
                            act.wait_ge(s_pt, t - NP + 1)
                        for j in range(4):
                            last = act.activation(prob[t % NP][:, j, :], sc_bank[t % NSC][:, j * P:(j + 1) * P], ACT.Exp,
                                                  bias=negmax[:, t % NS, j:j + 1], accum_out=total[:, t % NS, j:j + 1])
                        last.then_inc(s_exp, 1)
                    if half_in_ev(t + 3) is not None:
                        h = half_in_ev(t + 3)
                        b = h // 2
                        act.wait_ge(s_pv, 4 * h + 4)
                        if b >= 2:
                            act.wait_ge(s_o, 2 * (b - 1))
                        act.activation(oT_hi[b % 2][:, 4 * (h % 2):4 * (h % 2) + 4, :].rearrange("p a b -> p (a b)"),
                                       pv_bank[h % 2][:], ACT.Copy).then_inc(s_ohi, 1)
                    if chunk_in_dn(t) is not None:
                        n = chunk_in_dn(t)
                        act.wait_ge(s_dn[n % 2], 16 * (n // 2 + 1))
                        act.activation(dn_hi[:, n, :], dn_raw[n % 2][:], ACT.Copy).then_inc(s_dhi, 1)

            @block.vector
            def _(dve):
                for i in range(KQ):
                    last = dve.memset(k_in[i][:].bitcast(F32), 0.0)
                last.then_inc(s_zero, 1)
                for t in range(STEPS):
                    if t < QUADS:
                        dve.wait_ge(s_score, t + 1)
                        dve.tensor_reduce(negmax[:, t % NS, :], sc_bank[t % NSC][:].rearrange("p (j k) -> p j k", j=4),
                                          AX.X, ALU.max, negate=True).then_inc(s_max, 1)
                    if t == 2:
                        dve.wait_ge(s_bo, 16)
                        dve.tensor_scalar(bo_row[:], bo_row[:], gates[:, 0:1], None, ALU.mult).then_inc(s_bog, 1)
                    if 2 <= t < QUADS + 2:
                        n = (t - 2) % NS
                        dve.wait_ge(s_exp, t - 1)
                        dve.reciprocal(rec[:, n, :], total[:, n, :]).then_inc(s_rec, 1)
                    if T_LAG <= t < QUADS + T_LAG:
                        u = t - T_LAG
                        dve.wait_ge(s_pt, u + 1)
                        if u // 2 >= 2:
                            dve.wait_ge(s_pv, u // 2 - 1)
                        dve.tensor_copy(probT[u // 2 % 2][:, 4 * (u % 2):4 * (u % 2) + 4, :].rearrange("p a b -> p (a b)"),
                                        pt_bank[u % 2][:]).then_inc(s_ptc, 1)
                    if half_in_ev(t) is not None:
                        h = half_in_ev(t)
                        b, part = h // 2, slice(4 * (h % 2), 4 * (h % 2) + 4)
                        dve.wait_ge(s_ohi, h + 1)
                        dve.tensor_tensor(oT_lo[b % 2][:, part, :].rearrange("p a b -> p (a b)"), pv_bank[h % 2][:],
                                          oT_hi[b % 2][:, part, :].rearrange("p a b -> p (a b)").bitcast(F32),
                                          ALU.subtract).then_inc(s_olo, 1)
                    done = chunk_in_o(t - 1)
                    if done and done[2] == KC - 1:
                        b, half, _ = done
                        cols = slice(half * HALF, (half + 1) * HALF)
                        dve.wait_ge(s_o, 2 * b + half + 1)
                        dve.wait_ge(s_xbo, 2 * b + half + 1)
                        if half == 0 and b >= 2:
                            dve.wait_ge(s_x2st[b % 2], 16 * (b // 2))
                        dve.scalar_tensor_tensor(out=x2[b % 2][:, cols], in0=o_bank[:], scalar=gates[:, 0:1],
                                                 in1=xb[b % 2][:, cols], op0=ALU.mult, op1=ALU.add).then_inc(s_x2, 1)
                    done = chunk_in_o(t - 2)
                    if done and done[2] == KC - 1:
                        b, half, _ = done
                        dve.wait_ge(s_x2, 2 * b + half + 1)
                        dve.bn_stats(ln2_stats[:, b, half, :], x2[b % 2][:, half * HALF:(half + 1) * HALF])

            @block.gpsimd
            def _(pool):
                for t in range(QUADS + O_AT):
                    if t < QUADS:
                        pool.wait_ge(s_rec, t + 1)
                        pool.tensor_tensor(prob[t % NP][:], prob[t % NP][:],
                                           rec[:, t % NS, :].unsqueeze(2).to_broadcast([P, 4, P]), ALU.mult).then_inc(s_norm, 1)
                    b, step = (t - 18) // QB, (t - 18) % QB
                    if t >= 18 and b < NB and step in (0, 4):
                        half = step // 4
                        cols = slice(half * HALF, (half + 1) * HALF)
                        if half == 0:
                            pool.wait_ge(s_bog, 1)
                            pool.wait_ge(s_xb[b % 2], 16 * (b // 2 + 1))
                        pool.tensor_tensor(xb[b % 2][:, cols], xb[b % 2][:, cols], bo_row[:, cols], ALU.add).then_inc(s_xbo, 1)
                    n = chunk_in_dn(t - 1)
                    if n is not None:
                        pool.wait_ge(s_dhi, n + 1)
                        pool.tensor_tensor(dn_lo[:, n, :], dn_raw[n % 2][:], dn_hi[:, n, :].bitcast(F32),
                                           ALU.subtract).then_inc(s_dlo, 1)

        with ExitStack() as st, nc.Block() as block:
            wg_hi, wg_lo = w1_hi, w1_lo
            up_hi, up_lo = (sb(n, [P, LC, D], F32R, st) for n in ("up_hi", "up_lo"))
            yT_hi = sb("yT_hi", [P, GB, KC, P], F32R, st)
            yT_lo = sb("yT_lo", [P, GB, KC, P], F32R, st)
            h_hi = sb("h_hi", [P, LC, GT], F32R, st)
            h_lo = sb("h_lo", [P, LC, GT], F32R, st)
            NX = 5
            raw = [sb(f"raw_d{i}", [P, D], F32, st) for i in range(2)]
            xm = [sb(f"xm{i}", [P, D], F32, st) for i in range(NX - 1)] + [raw[0]]
            yn = sb("yn", [P, D], F32, st)
            keysT = sb("keysT", [NK, NE], F32, st)
            key_w = sb("key_w", [P, KC, NE], F32, st)
            mv = sb("mv_d", [P, NB, 2], F32, st)
            root = sb("root_d", [P, NB], F32, st)
            rstd = sb("rstd_d", [P, NB], F32, st)
            tmp = sb("tmp_d", [P, NB], F32, st)
            msum = sb("msum", [P, KC, GB], F32, st)
            score = sb("score", [GB, NE], F32, st)
            smax = sb("smax", [GB, 1], F32, st)
            expo = sb("expo", [GB, NE], F32, st)
            ssum = sb("ssum", [GB, 1], F32, st)
            coef = sb("coef", [GB, NE], F32, st)
            coefw = yn[0:GB, 0:NE * R].rearrange("b (e r) -> b e r", e=NE)
            coefc = sb("coefc", [P, LC, GB], F32, st)
            s_raw = [sem(f"s_raw_d{i}") for i in range(2)]
            s_xm = [sem(f"s_xm{i}") for i in range(NX)]
            s_ost = [sem(f"s_ost{i}") for i in range(NX)]
            s_statd, s_rootd, s_yn, s_small, s_smalle = (sem(n) for n in ("s_statd", "s_rootd", "s_yn", "s_small", "s_smalle"))
            line, plan = new_line("d"), []
            ring = RawRing(line, plan, raw, s_raw)
            t_end, out_end = {}, {}

            def load_xm(b):
                slot = b % NX
                free = out_end[b - NX] if b >= NX else 0

                def load(sp):
                    if free:
                        sp.wait_ge(s_ost[slot], 16 * (b // NX))
                    if b == NX - 1:
                        sp.wait_ge(line.emptied, weights_end)
                    sp.dma_start(xm[slot][:], x_mid[b * P:(b + 1) * P, :]).then_inc(s_xm[slot], 16)
                plan.append((free + 0.8 if free else weights_end + 0.1 if b == NX - 1 else -1 + 0.1 * b, load))

            def all_stats(dve):
                for b in range(NB):
                    last = dve.bn_aggr(mv[:, b, :], ln2_stats[:, b, :, :])
                link(last)
                link(dve.tensor_scalar(mv[:, :, 1:2], mv[:, :, 1:2], EPS, None, ALU.add))
                dve.sem_inc(s_statd, 1)

            def all_roots(act):
                act.wait_ge(s_statd, 1)
                act.activation(root[:], mv[:, :, 1:2].rearrange("p a b -> p (a b)"), ACT.Sqrt).then_inc(s_rootd, 1)

            def y_jobs(b, spread_end=0):
                def normalise(dve):
                    if b == 0:
                        dve.wait_ge(s_rootd, 1)
                        inverse_root(dve, mv[:, :, 1:2].rearrange("p a b -> p (a b)"), root[:], rstd[:], tmp[:])
                    dve.wait_ge(s_xm[b % NX], 16 * (b // NX + 1))
                    if b:
                        line.wait_filled(dve, t_end[b - 1])
                    if b and b % GB == 0:
                        line.wait_filled(dve, spread_end)
                    dve.tensor_scalar(yn[:], xm[b % NX][:], mv[:, b, 0:1], rstd[:, b:b + 1],
                                      ALU.subtract, ALU.mult).then_inc(s_yn, 1)
                load_xm(b)
                i = b % GB
                t_end[b] = transpose_jobs(line, yn, lambda pe: pe.wait_ge(s_yn, b + 1),
                                          yT_hi[:, i, :, :], yT_lo[:, i, :, :], sums=msum[:, :, i:i + 1], dve_pre=normalise)

            def key_jobs():
                slot, landed = ring.take(lora_keys)
                end = line.add(Job(
                    lambda bank: nc.tensor.transpose(bank[:, 0:NE], raw[slot][0:NE, 0:NK], ident[0:NE, 0:NE]),
                    lambda bank: nc.vector.tensor_copy(keysT[:], bank[:, 0:NE]), pe_wait=landed))
                ring.release(slot, end)
                slot2, landed2 = ring.take(w_key)

                def pe_fn(bank):
                    for k in range(KC):
                        last = nc.tensor.matmul(bank[:, k * NE:(k + 1) * NE], raw[slot2][:, k * P:(k + 1) * P], keysT[:],
                                                start=True, stop=True)
                    return last
                end = line.add(Job(pe_fn, lambda bank: nc.vector.tensor_copy(key_w[:].rearrange("p k e -> p (k e)"),
                                                                             bank[:, 0:KC * NE]),
                                   pe_wait=landed2, reads=end))
                ring.release(slot2, end)
                return end

            def up_chunk(k):
                up_rows = lora_up.rearrange("e r o -> (e r) o")
                slot, landed = ring.take(up_rows[k * P:(k + 1) * P, :])
                end = line.add(Job(
                    None, lambda bank: nc.vector.tensor_tensor(up_lo[:, k, :], raw[slot][:], up_hi[:, k, :].bitcast(F32),
                                                               ALU.subtract),
                    act=lambda bank: nc.scalar.activation(up_hi[:, k, :], raw[slot][:], ACT.Copy),
                    act_wait=landed, dve_wait=landed))
                ring.release(slot, end)
                return end

            def expert_jobs(g):
                def score_pe(bank):
                    for k in range(KC):
                        last = nc.tensor.matmul(bank[0:GB, 0:NE], msum[:, k, :], key_w[:, k, :], start=(k == 0), stop=(k == KC - 1))
                    return last

                def score_dve(bank):
                    link(nc.vector.tensor_reduce(smax[:], bank[0:GB, 0:NE], AX.X, ALU.max, negate=True))
                    link(nc.vector.tensor_scalar(score[:], bank[0:GB, 0:NE], smax[:, 0:1], None, ALU.add))
                    nc.vector.sem_inc(s_small, 1)
                    nc.vector.wait_ge(s_smalle, g + 1)
                    link(nc.vector.reciprocal(ssum[:], ssum[:]))
                    link(nc.vector.tensor_scalar(coef[:], expo[:], ssum[:, 0:1], None, ALU.mult))
                    return nc.vector.tensor_copy(coefw, coef[:].unsqueeze(2).to_broadcast([GB, NE, R]))
                end = line.add(Job(score_pe, score_dve, reads=max(t_end[g * GB + GB - 1], key_end),
                                   act_pre=lambda act: (
                    act.wait_ge(s_small, g + 1),
                    act.activation(expo[:], score[:], ACT.Exp, scale=1.0 / (S * NK ** 0.5), accum_out=ssum[:, 0:1])
                    .then_inc(s_smalle, 1))))

                def spread_pe(bank):
                    for c in range(LC):
                        last = nc.tensor.matmul(bank[:, c * GB:(c + 1) * GB], yn[0:GB, c * P:(c + 1) * P],
                                                ident[0:GB, 0:GB], start=True, stop=True)
                    return last
                return line.add(Job(spread_pe, lambda bank: nc.vector.tensor_copy(coefc[:].rearrange("p c b -> p (c b)"),
                                                                                  bank[:, 0:LC * GB]), reads=end))

            def h_job(g, c, coef_end):
                def pe_fn(bank):
                    return three_products(
                        bank[:], lambda k: (dn_hi[:, k, c * P:(c + 1) * P], dn_lo[:, k, c * P:(c + 1) * P]),
                        lambda k: (yT_hi[:, :, k, :], yT_lo[:, :, k, :]), range(KC))

                def hi_fn(bank):
                    for i in range(GB):
                        tok = slice(i * P, (i + 1) * P)
                        last = nc.scalar.activation(h_hi[:, c, tok], bank[:, tok], ACT.Copy, scale=coefc[:, c, i:i + 1])
                    return last

                def lo_fn(bank):
                    for i in range(GB):
                        tok = slice(i * P, (i + 1) * P)
                        last = nc.vector.scalar_tensor_tensor(
                            out=h_lo[:, c, tok], in0=bank[:, tok], scalar=coefc[:, c, i:i + 1],
                            in1=h_hi[:, c, tok].bitcast(F32), op0=ALU.mult, op1=ALU.subtract)
                    return last
                return line.add(Job(pe_fn, lo_fn, act=hi_fn, reads=t_end[g * GB + GB - 1],
                                    act_wait=lambda act: act.wait_ge(line.emptied, coef_end)))

            def out_job(b, half, h_end):
                i, cols = b % GB, slice(half * HALF, (half + 1) * HALF)

                def pe_fn(bank):
                    tok = slice(i * P, (i + 1) * P)
                    return three_products(
                        bank[:],
                        lambda k: (yT_hi[:, i, k, :], yT_lo[:, i, k, :]) if k < KC
                        else (h_hi[:, k - KC, tok], h_lo[:, k - KC, tok]),
                        lambda k: (wg_hi[:, k, cols], wg_lo[:, k, cols]) if k < KC
                        else (up_hi[:, k - KC, cols], up_lo[:, k - KC, cols]),
                        range(KC + LC))
                part = xm[b % NX][:, cols]
                out_end[b] = line.add(Job(
                    pe_fn, lambda bank: nc.vector.scalar_tensor_tensor(
                        out=part, in0=bank[:], scalar=gates[:, 1:2], in1=part, op0=ALU.mult, op1=ALU.add),
                    reads=max(h_end, weights_end)))

            def store_out(b):
                end = out_end[b]

                def store(sp):
                    sp.wait_ge(line.emptied, end)
                    sp.dma_start(out_t[b * P:(b + 1) * P, :], xm[b % NX][:]).then_inc(s_ost[b % NX], 16)
                plan.append((end + 0.6, store))

            key_end = key_jobs()
            line.jobs[0].dve_pre, line.jobs[0].act_pre = all_stats, all_roots
            for b in range(GB):
                weight_chunk(line, ring, w_org, b, wg_hi, wg_lo)
                y_jobs(b)
            for c in range(GB, KC):
                weights_end, _ = weight_chunk(line, ring, w_org, c, wg_hi, wg_lo)
            for k in range(LC):
                weights_end = up_chunk(k)
            for g in range(NG):
                coef_end = expert_jobs(g)
                for c in range(LC):
                    h_end = h_job(g, c, coef_end)
                for b in range(g * GB, (g + 1) * GB):
                    out_job(b, 0, h_end)
                    out_job(b, 1, h_end)
                    store_out(b)
                    if g + 1 < NG:
                        y_jobs(b + GB, coef_end)

            def stores_end(sp):
                for i in range(NX):
                    sp.wait_ge(s_ost[i], 16 * len(range(i, NB, NX)))
            run_phase(block, line, plan, stores_end)


_INS = ['x', 'ctx_4096', 'g_xattn', 'g_ffn', 'L0_xattn_Wq', 'L0_xattn_bq', 'L0_xattn_Wk', 'L0_xattn_bk',
        'L0_xattn_Wv', 'L0_xattn_bv', 'L0_xattn_interference', 'L0_xattn_amp', 'L0_xattn_Wo', 'L0_xattn_bo',
        'L0_ffn_W_org', 'L0_ffn_lora_down', 'L0_ffn_lora_up', 'L0_ffn_lora_keys', 'L0_ffn_Wq']


def kernel(**inputs):
    import numpy as np
    import concourse.bacc as bacc
    from concourse.bass_utils import run_bass_kernel_spmd

    nc = bacc.Bacc("TRN2", target_bir_lowering=False, num_devices=1)
    arrays, args = {}, []
    for name in _INS:
        a = np.ascontiguousarray(inputs[name])
        arrays[f"in_{name}"] = a
        args.append(nc.dram_tensor(f"in_{name}", a.shape, mybir.dt.from_np(a.dtype), kind="ExternalInput").ap())
    args.append(nc.dram_tensor("out_x", inputs['x'].shape, F32, kind="ExternalOutput").ap())
    build(nc, *args)
    r = run_bass_kernel_spmd(nc, [arrays], core_ids=[0])
    return r.results[0]["out_x"]
```

```python
from contextlib import ExitStack

import concourse.bass as bass
from concourse import mybir

F32 = mybir.dt.float32
F32R = mybir.dt.float32r
ALU = mybir.AluOpType
ACT = mybir.ActivationFunctionType
AX = mybir.AxisListType

P = 128
EPS = 1e-5


class Job:

    def __init__(self, pe, dve, act=None, reads=0, pe_wait=None, act_wait=None, dve_wait=None,
                 act_pre=None, dve_pre=None):
        self.pe, self.dve, self.act, self.reads = pe, dve, act, reads
        self.pe_wait, self.act_wait, self.dve_wait = pe_wait, act_wait, dve_wait
        self.act_pre, self.dve_pre = act_pre, dve_pre


class Line:

    def __init__(self, banks, filled, scaled, emptied):
        self.banks, self.jobs = banks, []
        self.filled, self.scaled, self.emptied = filled, scaled, emptied

    def add(self, job):
        self.jobs.append(job)
        return len(self.jobs)

    def bank(self, n):
        return self.banks[n % len(self.banks)]

    def wait_filled(self, eng, end):
        eng.wait_ge(self.filled, sum(1 for job in self.jobs[:end] if job.pe))

    def run_tensor(self, pe):
        ring = len(self.banks)
        for n, job in enumerate(self.jobs):
            need = max(n + 1 - ring, job.reads, 0)
            if job.pe:
                if need:
                    pe.wait_ge(self.emptied, need)
                if job.pe_wait:
                    job.pe_wait(pe)
                job.pe(self.bank(n)).then_inc(self.filled, 1)

    def run_scalar(self, act):
        for n, job in enumerate(self.jobs):
            if job.act_pre:
                job.act_pre(act)
            if job.act:
                if job.pe:
                    self.wait_filled(act, n + 1)
                if job.act_wait:
                    job.act_wait(act)
                job.act(self.bank(n)).then_inc(self.scaled, 1)

    def run_vector(self, dve):
        scaled = 0
        for n, job in enumerate(self.jobs):
            if job.dve_pre:
                job.dve_pre(dve)
            if job.act:
                scaled += 1
                dve.wait_ge(self.scaled, scaled)
            else:
                self.wait_filled(dve, n + 1)
            if job.dve_wait:
                job.dve_wait(dve)
            job.dve(self.bank(n)).then_inc(self.emptied, 1)


def build(nc, x, ctx_in, g_xattn, g_ffn, wq, bq, wk, bk, wv, bv, interference, amp, wo, bo,
          w_org, lora_down, lora_up, lora_keys, w_key, out):
    NB, S, D = x.shape
    NH, NM, _ = interference.shape
    DK = D // (NH * NM)
    HM = NH * NM
    NE, _, R = lora_down.shape
    NK = w_key.shape[0]
    T = NB * S
    KC = D // P
    GB = 4
    NG = NB // GB
    GT = GB * S
    HALF = 512
    LC = NE * R // P
    STACK = 3 * DK
    OCT = P // DK
    NOCT = HM // OCT
    PAIRS = HM // 2
    assert S == P and OCT == 8 and T % GT == 0

    x_t = x.rearrange("b s d -> (b s) d")
    ctx_t = ctx_in.rearrange("b s d -> (b s) d")
    out_t = out.rearrange("b s d -> (b s) d")

    k_stack = nc.dram_tensor("k_stack", (HM, 3, DK, T), F32, kind="Internal").ap()
    q_stack = nc.dram_tensor("q_stack", (HM, 3, DK, T), F32, kind="Internal").ap()
    v_pad = nc.dram_tensor("v_pad", (T, PAIRS * 2 * 32), F32, kind="Internal").ap()
    x_mid = nc.dram_tensor("x_mid", (T, D), F32, kind="Internal").ap()

    top = ExitStack()
    with top:
        def sem(name):
            return top.enter_context(nc.semaphore(name))

        def sb(name, shape, dt=F32, stack=top):
            return stack.enter_context(nc.sbuf_tensor(name, shape, dt))

        def arriving(name, rows, before=0):
            with ExitStack() as overlaid:
                if before:
                    sb(f"{name}_before", [P, before], stack=overlaid)
                tile = sb(name, [P, rows, D], stack=overlaid)
            return [tile[:, j, :] for j in range(rows)]

        banks = [top.enter_context(nc.psum_tensor(f"bank{i}", [P, HALF], F32)) for i in range(8)]

        ident = sb("ident", [P, P])
        gates = sb("gates", [P, 2])
        s_const = sem("s_const")
        s_chain = sem("s_chain")
        chain = [0]

        def link(ins):
            chain[0] += 1
            ins.then_inc(s_chain, 1)
            nc.vector.wait_ge(s_chain, chain[0])

        def split_hi(hi, bank_ap, **kw):
            return nc.scalar.activation(hi, bank_ap, ACT.Copy, **kw)

        def split_lo(lo, bank_ap, hi):
            return nc.vector.tensor_tensor(lo, bank_ap, hi.bitcast(F32), ALU.subtract)

        def three_products(bank_ap, station, moving, chunks):
            last = None
            for i, k in enumerate(chunks):
                (sh, sl), (mh, ml) = station(k), moving(k)
                nc.tensor.matmul(bank_ap, sh, mh, start=(i == 0), stop=False)
                nc.tensor.matmul(bank_ap, sh, ml, start=False, stop=False)
                last = nc.tensor.matmul(bank_ap, sl, mh, start=False, stop=(i == len(chunks) - 1))
            return last

        place_a, place_b, place_c = (sb(f"place_{n}", [P, KC, D], F32R) for n in "abc")

        def half_place(place, i, width):
            part = place[:, i * KC // 2:(i + 1) * KC // 2, :]
            return part.rearrange("p a (b c) -> p (a b) c", c=width)

        tin = arriving("tin", 2)
        with ExitStack() as overlaid:
            h_lo = sb("h_lo", [P, LC, GT], F32R, overlaid)
        first_k = sb("first_k", [2 * STACK, 4, 2, P], F32R)
        first_q = [sb(f"first_q{i}", [2 * STACK, 4, P], F32R) for i in range(2)]
        KQ = 4
        s_kq = [sem(f"s_kq{i}") for i in range(KQ)]

        def load_kq(sp, o, k_tile, q_tile, landed):
            b, first = o // NOCT, (o % NOCT) * OCT
            tok = slice(b * P, (b + 1) * P)
            sp.dma_start(
                q_tile[:].bitcast(F32),
                q_stack[first:first + OCT, :, :, tok].rearrange("(p a) s d t -> (a s d) p t", a=2)
            ).then_inc(landed, 16)
            for a in range(2):
                sp.dma_start(
                    k_tile[a * STACK:(a + 1) * STACK, :, a, :].bitcast(F32),
                    k_stack[first + a:first + OCT:2, :, :, tok].rearrange("p s d t -> (s d) p t")
                ).then_inc(landed, 16)

        proj = ExitStack()
        w0_hi, w0_lo = (sb(n, [P, KC, D], F32R, proj) for n in ("w0_hi", "w0_lo"))
        mix = sb("mix", [P, KC, P], stack=proj)
        bias_mixed = sb("bias_mixed", [P, 2, KC], stack=proj)
        bv_row = sb("bv_row", [P, D], stack=proj)
        bcol = sb("bcol", [P, 3, KC], stack=proj)
        NRAW = 3
        raw = [sb(f"raw{i}", [P, D], F32, proj) for i in range(NRAW)]
        s_raw = [sem(f"s_raw{i}") for i in range(NRAW)]
        s_tin = [sem(f"s_tin{i}") for i in range(2)]

        with ExitStack() as st, nc.Block() as block:
            jm = sb("jm", [NM, NH, NM], stack=st)
            amp4 = sb("amp4", [NM, 1], stack=st)
            braw = sb("braw", [3 * KC, P], stack=st)
            graw = sb("graw", [P, 2], stack=st)
            rowsel = sb("rowsel", [NM, P // NM, NM], stack=st)
            jrow = sb("jrow", [P, NH, NM], stack=st)
            group = sb("group", [P, P // NM], stack=st)
            s_in, s_bias, s_id, s_ready, s_mm, s_g = (sem(n) for n in ("s_in", "s_bias", "s_id", "s_ready", "s_mm", "s_g"))

            @block.sync
            def _(sp):
                with nc.allow_non_contiguous_dma(reason="a few hundred small elements"):
                    sp.dma_start(jm[:], interference.rearrange("h i j -> i h j")).then_inc(s_in, 16)
                    sp.dma_start(amp4[:], amp.partition_broadcast(NM)).then_inc(s_in, 16)
                    sp.dma_start(raw[0][:], wk[0:P, :]).then_inc(s_raw[0], 16)
                    sp.dma_start(graw[:, 0:1], g_xattn.partition_broadcast(P)).then_inc(s_bias, 16)
                    sp.dma_start(graw[:, 1:2], g_ffn.partition_broadcast(P)).then_inc(s_bias, 16)
                    for i, b in enumerate((bk, bq, bv)):
                        sp.dma_start(braw[i * KC:(i + 1) * KC, :],
                                     b.rearrange("(c i) -> c i", i=P)).then_inc(s_bias, 16)
                for i in range(2):
                    sp.dma_start(tin[i], ctx_t[i * P:(i + 1) * P, :]).then_inc(s_tin[i], 16)
                for i in range(1, NRAW):
                    sp.dma_start(raw[i][:], wk[i * P:(i + 1) * P, :]).then_inc(s_raw[i], 16)

            @block.gpsimd
            def _(pool):
                pool.memset(ident[:], 0.0).then_inc(s_id, 1)
                pool.wait_ge(s_id, 1)
                pool.affine_select(out=ident[:], in_=ident[:], compare_op=ALU.not_equal, fill=1.0, base=0,
                                   pattern=[[-1, P]], channel_multiplier=1).then_inc(s_id, 1)

            @block.scalar
            def _(act):
                act.wait_ge(s_bias, 5 * 16)
                act.activation(gates[:], graw[:], ACT.Tanh).then_inc(s_g, 1)

            @block.vector
            def _(dve):
                dve.wait_ge(s_id, 2)
                dve.tensor_copy(rowsel[:], ident[0:NM, 0:NM].unsqueeze(1).to_broadcast([NM, P // NM, NM]))
                dve.tensor_reduce(group[:], ident[:].rearrange("p (g f) -> p g f", f=NM), AX.X, ALU.add)
                dve.wait_ge(s_in, 2 * 16)
                link(dve.tensor_scalar(jm[:], jm[:], amp4[:, 0:1], 0.1, ALU.mult, ALU.mult))
                link(dve.tensor_tensor(jm[:], jm[:],
                                       ident[0:NM, 0:NM].unsqueeze(1).to_broadcast([NM, NH, NM]), ALU.add))
                dve.sem_inc(s_ready, 1)
                dve.wait_ge(s_mm, 1)
                link(dve.tensor_copy(jrow[:].rearrange("p h m -> p (h m)"), banks[0][:, 0:HM]))
                for c in range(KC):
                    for h2 in range(2):
                        width = P // 2
                        dst = mix[:, c, h2 * width:(h2 + 1) * width].rearrange("p (m d) -> p m d", m=NM)
                        dve.tensor_tensor(
                            dst, jrow[:, 2 * c + h2, :].unsqueeze(2).to_broadcast([P, NM, DK]),
                            group[:, h2 * DK:(h2 + 1) * DK].unsqueeze(1).to_broadcast([P, NM, DK]), ALU.mult)
                dve.wait_ge(s_mm, 2)
                dve.tensor_copy(bcol[:].rearrange("p a c -> p (a c)"), banks[1][:, 0:3 * KC])
            @block.tensor
            def _(pe):
                pe.wait_ge(s_ready, 1)
                pe.matmul(banks[0][:, 0:HM], rowsel[:].rearrange("m g f -> m (g f)"),
                          jm[:].rearrange("i h j -> i (h j)"), start=True, stop=True).then_inc(s_mm, 1)
                pe.wait_ge(s_bias, 5 * 16)
                pe.transpose(banks[1][:, 0:3 * KC], braw[:], ident[0:3 * KC, 0:3 * KC]).then_inc(s_mm, 1)

        class RawRing:

            def __init__(self, line, plan, tiles, sems, preloaded=0):
                self.line, self.plan, self.tiles, self.sems = line, plan, tiles, sems
                self.uses, self.last, self.preloaded = 0, {}, preloaded

            def take(self, src, ahead=0.5):
                slot, n = self.uses % len(self.tiles), self.uses // len(self.tiles) + 1
                free = self.last.get(slot, 0)

                def load(sp):
                    if free:
                        sp.wait_ge(self.line.emptied, free)
                    dst = self.tiles[slot][0:src.shape[0], 0:src.shape[-1]]
                    sp.dma_start(dst, src).then_inc(self.sems[slot], 16)

                if self.uses >= self.preloaded:
                    self.plan.append((free - ahead, load))
                self.uses += 1
                return slot, lambda eng: eng.wait_ge(self.sems[slot], 16 * n)

            def release(self, slot, end):
                self.last[slot] = end

        def weight_chunk(line, ring, w, c, w_hi, w_lo, mixed=None, reorder=None, reads=0):
            slot, landed = ring.take(w[c * P:(c + 1) * P, :])

            def reorder_inputs(act):
                tiles, done, ends = reorder
                landed(act)
                if c >= len(tiles):
                    line.wait_filled(act, ends[c - len(tiles)])
                act.activation(tiles[c % len(tiles)].rearrange("p (h m d) -> p h m d", h=NH, m=NM),
                               ring.tiles[slot][:].rearrange("p (h d m) -> p h m d", h=NH, m=NM), ACT.Copy).then_inc(done, 1)

            for half in range(2):
                def pe_fn(bank, half=half):
                    src = reorder[0][c % len(reorder[0])] if reorder else ring.tiles[slot]
                    for q in range(4):
                        rows = src[:, (4 * half + q) * P:(4 * half + q + 1) * P]
                        dst = bank[:, q * P:(q + 1) * P]
                        if mixed is not None:
                            last = nc.tensor.matmul(dst, rows, mixed[:, c, :], start=True, stop=True)
                        else:
                            last = nc.tensor.transpose(dst, rows, ident[:])
                    return last

                hi = w_hi[:, 4 * half:4 * half + 4, c * P:(c + 1) * P]
                lo = w_lo[:, 4 * half:4 * half + 4, c * P:(c + 1) * P]
                end = line.add(Job(
                    pe_fn, lambda bank, hi=hi, lo=lo: split_lo(lo, bank[:].rearrange("p (q r) -> p q r", q=4), hi),
                    act=lambda bank, hi=hi: split_hi(hi, bank[:].rearrange("p (q r) -> p q r", q=4)),
                    pe_wait=(lambda pe: pe.wait_ge(reorder[1], c + 1)) if reorder else landed, reads=reads))
            ring.release(slot, end)
            if reorder:
                reorder[2][c] = end
            return end, reorder_inputs

        def transpose_jobs(line, tile, wait, hi, lo, sums=None):
            for half in range(2):
                def pe_fn(bank, half=half):
                    for q in range(4):
                        k = 4 * half + q
                        last = nc.tensor.transpose(bank[:, q * P:(q + 1) * P], tile[:, k * P:(k + 1) * P], ident[:])
                    return last

                part = slice(4 * half, 4 * half + 4)
                flat_hi = hi[:, part, :].rearrange("p a b -> p (a b)")
                flat_lo = lo[:, part, :].rearrange("p a b -> p (a b)")

                def empty(bank, part=part, flat_hi=flat_hi, flat_lo=flat_lo):
                    if sums is not None:
                        nc.vector.tensor_reduce(sums[:, part, :], bank[:].rearrange("p (q s) -> p q s", q=4),
                                                AX.X, ALU.add)
                    return split_lo(flat_lo, bank[:], flat_hi)
                end = line.add(Job(pe_fn, empty, act=lambda bank, flat_hi=flat_hi: split_hi(flat_hi, bank[:]),
                                   pe_wait=wait))
            return end

        def inverse_root(dve, var, root, rstd, tmp):
            link(dve.reciprocal(rstd, root))
            link(dve.tensor_tensor(tmp, rstd, rstd, ALU.mult))
            link(dve.tensor_tensor(tmp, tmp, var, ALU.mult))
            link(dve.tensor_scalar(tmp, tmp, -0.5, 1.5, ALU.mult, ALU.add))
            link(dve.tensor_tensor(rstd, rstd, tmp, ALU.mult))

        class LayerNorm:

            def __init__(self, tag, stack):
                self.stats = sb(f"ln_stats_{tag}", [P, 2, 6], F32, stack)
                self.mv = sb(f"ln_mv_{tag}", [P, 2], F32, stack)
                self.root, self.rstd, self.tmp = (sb(f"ln_{n}_{tag}", [P, 1], F32, stack) for n in ("root", "rstd", "tmp"))
                self.s_stat, self.s_root, self.s_done = (sem(f"s_ln_{n}_{tag}") for n in ("stat", "root", "done"))

            def vector_stages(self, n, tile, landed):
                def first_half(dve):
                    if n:
                        dve.wait_ge(self.s_done, n)
                    landed(dve)
                    dve.bn_stats(self.stats[:, 0, :], tile[:, 0:HALF])

                def variance(dve):
                    link(dve.bn_stats(self.stats[:, 1, :], tile[:, HALF:D]))
                    link(dve.bn_aggr(self.mv[:], self.stats[:]))
                    dve.tensor_scalar(self.mv[:, 1:2], self.mv[:, 1:2], EPS, None, ALU.add).then_inc(self.s_stat, 1)

                def inverse(dve):
                    dve.wait_ge(self.s_root, n + 1)
                    inverse_root(dve, self.mv[:, 1:2], self.root[:], self.rstd[:], self.tmp[:])

                def normalise(dve):
                    dve.tensor_scalar(tile[:], tile[:], self.mv[:, 0:1], self.rstd[:, 0:1],
                                      ALU.subtract, ALU.mult).then_inc(self.s_done, 1)
                return first_half, variance, inverse, normalise

            def vector_steps(self, n, tile, landed):
                def pre(dve):
                    for stage in self.vector_stages(n, tile, landed):
                        stage(dve)
                return pre

            def scalar_step(self, n):
                def pre(act):
                    act.wait_ge(self.s_stat, n + 1)
                    act.activation(self.root[:], self.mv[:, 1:2], ACT.Sqrt).then_inc(self.s_root, 1)
                return pre

            def done(self, n):
                return lambda eng: eng.wait_ge(self.s_done, n + 1)

        def run_phase(block, line, plan, stores_end=None):
            @block.sync
            def _(sp):
                for _, step in sorted(plan, key=lambda e: e[0]):
                    step(sp)
                if stores_end:
                    stores_end(sp)

            @block.tensor
            def _(pe):
                line.run_tensor(pe)

            @block.scalar
            def _(act):
                line.run_scalar(act)

            @block.vector
            def _(dve):
                line.run_vector(dve)

        def new_line(tag):
            return Line(banks, sem(f"s_filled_{tag}"), sem(f"s_scaled_{tag}"), sem(f"s_emptied_{tag}"))

        with proj, ExitStack() as st, nc.Block() as block:
            cT_hi, cT_lo, odd_hi, odd_lo = (
                half_place(place, i, P).rearrange("p (i k) c -> p i k c", i=GB)
                for place in (place_a, place_b) for i in range(2))
            wv_hi, wv_lo, wo_hi, wo_lo = place_b, place_c, place_a, place_c
            stage_hi = [sb(f"stage_hi{i}", [P, GT], F32R, st) for i in range(2)]
            stage_lo = [sb(f"stage_lo{i}", [P, GT], F32R, st) for i in range(2)]
            v_out = [sb(f"v_out{i}", [P, PAIRS // 2, 2, 32], F32, st) for i in range(2)]
            reordered = [v[:].rearrange("p q a d -> p (q a d)") for v in v_out]
            norm = LayerNorm("x", st)
            s_stage = [sem(f"s_stage{i}") for i in range(2)]
            s_vst = [sem(f"s_vst{i}") for i in range(2)]
            s_reordered, s_third, s_cleared = sem("s_reordered"), sem("s_third"), sem("s_cleared")
            line, plan = new_line("a"), []
            ring = RawRing(line, plan, raw, s_raw, preloaded=NRAW)

            def x_place(g):
                return (cT_hi, cT_lo) if g % 2 == 0 else (odd_hi, odd_lo)

            t_end = {}

            def load_input(n):
                slot, free = n % 2, t_end.get(n - 2, 0)
                src = ctx_t[n * P:(n + 1) * P, :] if n < NB else x_t[(n - NB) * P:(n - NB + 1) * P, :]

                if n == 2:
                    plan.append((-1, lambda sp: sp.dma_start(reordered[1], src).then_inc(s_third, 16)))
                    return reordered[1], lambda eng: eng.wait_ge(s_third, 16)
                use = n // 2 + (slot == 1 or n < 2)

                def load(sp):
                    line.wait_filled(sp, free)
                    sp.dma_start(tin[slot], src).then_inc(s_tin[slot], 16)
                if n >= 2:
                    plan.append((free - 0.5, load))
                return tin[slot], lambda eng: eng.wait_ge(s_tin[slot], 16 * use)

            def ctx_jobs(b):
                tile, landed = load_input(b)
                t_end[b] = transpose_jobs(
                    line, tile, landed, cT_hi[:, b % GB, :, :], cT_lo[:, b % GB, :, :])

            def x_norm(b, job):
                n = NB + b
                job.dve_pre = norm.vector_steps(b, *load_input(n))
                job.act_pre = norm.scalar_step(b)

            def x_jobs(b):
                hi, lo = x_place(b // GB)
                t_end[NB + b] = transpose_jobs(line, tin[b % 2], norm.done(b), hi[:, b % GB, :, :], lo[:, b % GB, :, :])

            staged = [0]

            def projection_job(weight_end, input_end, hi_in, lo_in, bias, scratch, c, g, lo_section):
                slot, use = staged[0] % 2, staged[0] // 2
                staged[0] += 1
                hi, lo = stage_hi[slot], stage_lo[slot]

                def pe_fn(bank):
                    return three_products(
                        bank[:], lambda k: (w0_hi[:, k, c * P:(c + 1) * P], w0_lo[:, k, c * P:(c + 1) * P]),
                        lambda k: (hi_in[:, :, k, :], lo_in[:, :, k, :]), range(KC))

                def stage_free(act):
                    if use:
                        act.wait_ge(s_stage[slot], 48 * use)
                job = Job(
                    pe_fn,
                    lambda bank: nc.vector.scalar_tensor_tensor(
                        out=lo[:], in0=bank[:], scalar=bias, in1=hi[:].bitcast(F32), op0=ALU.add, op1=ALU.subtract),
                    act=lambda bank: nc.scalar.activation(hi[:], bank[:], ACT.Identity, bias=bias),
                    reads=max(input_end, weight_end), act_wait=stage_free)
                end = line.add(job)

                def store(sp):
                    sp.wait_ge(line.emptied, end)
                    for section in range(3):
                        src = lo if section == lo_section else hi
                        sp.dma_start(scratch[c * OCT:(c + 1) * OCT, section, :, g * GT:(g + 1) * GT],
                                     src[:].bitcast(F32)).then_inc(s_stage[slot], 16)
                plan.append((end + 0.6, store))
                return job

            def k_job(g, c):
                return projection_job(wk_end[c], t_end[g * GB + GB - 1], cT_hi, cT_lo, bias_mixed[:, 0, c:c + 1],
                                      k_stack, c, g, 2)

            def q_job(g, c):
                return projection_job(wq_end, t_end[NB + g * GB + GB - 1], *x_place(g), bias_mixed[:, 1, c:c + 1],
                                      q_stack, c, g, 1)

            def v_job(b, half):
                n = 2 * b + half
                slot, use = n % 2, n // 2
                gslot = b % GB
                cols = slice(half * HALF, (half + 1) * HALF)

                def pe_fn(bank):
                    return three_products(
                        bank[:], lambda k: (cT_hi[:, gslot, k, :], cT_lo[:, gslot, k, :]),
                        lambda k: (wv_hi[:, k, cols], wv_lo[:, k, cols]), range(KC))

                def empty(bank):
                    def by_pair(ap):
                        return ap.rearrange("p (q a d) -> p q a d", a=2, d=DK)
                    for a in range(2):
                        last = nc.vector.tensor_tensor(v_out[slot][:, :, a, a * DK:(a + 1) * DK],
                                                       by_pair(bank[:])[:, :, a, :],
                                                       by_pair(bv_row[:, cols])[:, :, a, :], ALU.add)
                    return last

                def stage_free(dve):
                    if use:
                        dve.wait_ge(s_vst[slot], 16 * use)
                job = Job(pe_fn, empty, reads=max(t_end[b], wv_end), dve_wait=stage_free)
                end = line.add(job)

                def store(sp):
                    sp.wait_ge(line.emptied, end)
                    width = PAIRS * 32
                    sp.dma_start(v_pad[b * P:(b + 1) * P, half * width:(half + 1) * width],
                                 v_out[slot][:].rearrange("p q a d -> p (q a d)")).then_inc(s_vst[slot], 16)
                plan.append((end + 0.6, store))
                return job

            def bias_jobs():
                spread = v_out[0][:].rearrange("p q a d -> p (q a d)").rearrange("p (c j) -> p c j", c=KC)

                def columns(bank):
                    for c in range(KC):
                        last = nc.tensor.matmul(bank[:, 2 * c:2 * c + 2], mix[:, c, :], bcol[:, 0:2, c], start=True, stop=True)
                    return last

                def take_columns(bank):
                    by_chunk = bank[:, 0:2 * KC].rearrange("p (c a) -> p a c", a=2)
                    nc.vector.tensor_copy(bias_mixed[:, 0, :], by_chunk[:, 0, :])
                    nc.vector.tensor_scalar(bias_mixed[:, 1, :], by_chunk[:, 1, :], DK ** -0.5, None, ALU.mult)
                    return nc.vector.tensor_copy(spread, bcol[:, 2, :].unsqueeze(2).to_broadcast([P, KC, P]))
                end = line.add(Job(columns, take_columns))
                for half in range(2):
                    def row(bank, half=half):
                        for q in range(4):
                            c = 4 * half + q
                            last = nc.tensor.matmul(bank[:, q * P:(q + 1) * P], spread[:, c, :], mix[:, c, :], start=True, stop=True)
                        return last
                    line.add(Job(row, lambda bank, half=half: nc.vector.tensor_copy(
                        bv_row[:, half * HALF:(half + 1) * HALF], bank[:]), reads=end))

            wk_end = {}

            def wk_chunk(c):
                wk_end[c], _ = weight_chunk(line, ring, wk, c, w0_hi, w0_lo, mixed=mix)

            for b in range(2):
                ctx_jobs(b)
            wk_chunk(0)
            bias_jobs()
            wk_chunk(1)
            ctx_jobs(2)
            wk_chunk(2)
            ctx_jobs(3)
            wk_chunk(3)
            for c in range(KC):
                job = k_job(0, c)
                if c == 0:
                    job.dve_pre = lambda dve: [link(dve.memset(v[:], 0.0)) for v in v_out]
                if c + 4 < KC:
                    wk_chunk(c + 4)
                wv_end, _ = weight_chunk(line, ring, wv, c, wv_hi, wv_lo, mixed=mix)
            for g in range(NG):
                for b in range(g * GB, (g + 1) * GB):
                    v_job(b, 0)
                    if g + 1 < NG:
                        v_job(b, 1)
                        ctx_jobs(b + GB)
                        continue
                    xb = b - g * GB
                    for c in (2 * xb, 2 * xb + 1):
                        wq_end, _ = weight_chunk(line, ring, wq, c, w0_hi, w0_lo, mixed=mix, reads=mix_scaled)
                    v_job(b, 1)
                    x_norm(xb, line.jobs[-4])
                    x_jobs(xb)
                if g + 1 < NG:
                    for c in range(KC):
                        job = k_job(g + 1, c)
                        if g + 2 == NG and c == 0:
                            def scale_mix(dve):
                                line.wait_filled(dve, wv_end)
                                link(dve.tensor_scalar(mix[:], mix[:], DK ** -0.5, None, ALU.mult))
                            job.dve_pre, mix_scaled = scale_mix, len(line.jobs)
            reorder = (reordered, s_reordered, {})

            def wo_chunk(c, carrier):
                _, reorder_inputs = weight_chunk(line, ring, wo, c, wo_hi, wo_lo, reorder=reorder)

                def v_stored(act):
                    for i in range(2):
                        act.wait_ge(s_vst[i], 16 * NB)
                    reorder_inputs(act)
                carrier.act_pre = reorder_inputs if c else v_stored

            for g in range(NG):
                for c in range(KC):
                    job = q_job(g, c)
                    if g + 1 < NG:
                        if c in (0, 2, 4, 5):
                            x_norm((g + 1) * GB + (0, 2, 4, 5).index(c), job)
                        if c in (1, 3, 5, 6):
                            x_jobs((g + 1) * GB + (1, 3, 5, 6).index(c))
                    elif c:
                        wo_chunk(c - 1, previous)
                    if (g, c) == (NG - 1, 1):
                        def zero_first(dve):
                            line.wait_filled(dve, t_end[2 * NB - 1])
                            dve.memset(first_k[:].bitcast(F32), 0.0).then_inc(s_cleared, 1)
                        job.dve_pre = zero_first

                        def load_first_oct(sp):
                            sp.wait_ge(s_cleared, 1)
                            sp.wait_ge(s_stage[0], 48 * (NG * KC // 2 + 1))
                            load_kq(sp, 0, first_k, first_q[0], s_kq[0])
                        plan.append((len(line.jobs) + 0.7, load_first_oct))
                    previous = job
            wo_chunk(KC - 1, previous)

            def stores_end(sp):
                for i in range(2):
                    sp.wait_ge(s_stage[i], 48 * NG * KC)
                    sp.wait_ge(s_vst[i], 16 * NB)
            run_phase(block, line, plan, stores_end)

        wo_hi, wo_lo = place_a, place_c
        dn_hi, dn_lo = (half_place(place_b, i, NE * R) for i in range(2))
        v_place = [sb(f"v_place{i}", [P, 2 * D]) for i in range(2)]
        h_tiles = arriving("h_hi_first", 2)
        h_hi = sb("h_hi", [P, LC, GT], F32R)
        yin, raw_d = ([v_place[i][:, j * D:(j + 1) * D] for j in range(2)] for i in range(2))
        first_y = yin + h_tiles
        s_raw_d = [sem(f"s_raw_d{i}") for i in range(2)]
        with ExitStack() as st, nc.Block() as block:
            q_in = first_q + [sb(f"q_in{i}", [2 * STACK, 4, P], F32R, st) for i in range(2, KQ)]
            k_in = [first_k] + [sb(f"k_in{i}", [2 * STACK, 4, 2, P], F32R, st) for i in range(1, KQ)]
            v_in = [v[:].rearrange("p (q a d) -> p q a d", a=2, d=32) for v in v_place]
            NP = 7
            prob = [sb(f"prob{i}", [P, 4, P], F32, st) for i in range(NP)]
            probT = [sb(f"probT{i}", [P, OCT, P], F32, st) for i in range(2)]
            NS = 8
            negmax = sb("negmax", [P, NS, 4], F32, st)
            total = sb("total", [P, NS, 4], F32, st)
            rec = sb("rec", [P, NS, 4], F32, st)
            oT_hi = [sb(f"oT_hi{i}", [P, NOCT, P], F32R, st) for i in range(2)]
            oT_lo = [sb(f"oT_lo{i}", [P, NOCT, P], F32R, st) for i in range(2)]
            bo_row = sb("bo_row", [P, D], F32, st)
            xb = [sb(f"xb{i}", [P, D], F32, st) for i in range(2)]
            x2 = [sb(f"x2_{i}", [P, D], F32, st) for i in range(2)]
            dn_raw = [sb(f"dn_raw{i}", [P, NE * R], F32, st) for i in range(2)]
            NSC = 3
            sc_bank, pt_bank, pv_bank, o_bank = banks[0:NSC], banks[3:5], banks[5:7], banks[7]

            norm = LayerNorm("c", st)
            s_first = [sem(f"s_first{i}") for i in range(GB)]
            s_v = [sem(f"s_v{i}") for i in range(2)]
            s_xb = [sem(f"s_xb{i}") for i in range(2)]
            s_x2st = [sem(f"s_x2st{i}") for i in range(2)]
            s_dn = [sem(f"s_dn{i}") for i in range(2)]
            s_zero = [sem(f"s_zero{i}") for i in range(2)]
            (s_score, s_max, s_exp, s_rec, s_norm, s_pt, s_ptc, s_pv, s_ohi, s_olo, s_o, s_x2,
             s_bo, s_bog, s_xbo, s_dhi, s_dlo) = (
                sem(n) for n in ("s_score", "s_max", "s_exp", "s_rec", "s_norm", "s_pt", "s_ptc",
                                 "s_pv", "s_ohi", "s_olo", "s_o", "s_x2", "s_bo", "s_bog", "s_xbo", "s_dhi", "s_dlo"))

            QUADS = NB * HM // 4
            QB = HM // 4
            OCTS = NB * NOCT
            T_LAG, PV_LAG, EV_AT, O_AT = 5, 8, 16, 26
            STEPS = QB * (NB - 1) + O_AT + 2 * KC + 1

            def oct_in_pv(t):
                o = (t - PV_LAG) // 2
                return o if t >= PV_LAG and t % 2 == 0 and o < OCTS else None

            def half_in_ev(t):
                h = (t - EV_AT) // 8
                return h if t >= EV_AT and (t - EV_AT) % 8 == 0 and h < 2 * NB else None

            def chunk_in_o(t):
                j = t - O_AT
                return (j // QB, j % QB // KC, j % KC) if 0 <= j < QB * NB else None

            DN_OCT, DN_STEP = 16, 30
            NORMS = [((2, 3, 0, 1)[j], QUADS + 4 * j + 2, QUADS + 4 * j + 4) for j in range(GB)]

            def out_bank(b, half):
                return sc_bank[half] if b == NB - 1 else o_bank

            def chunk_in_dn(t):
                n = (t - DN_STEP) // 4
                return n if t >= DN_STEP and (t - DN_STEP) % 4 == 0 and n < KC else None

            @block.sync
            def _(sp):
                def load_oct(o):
                    if 0 < o < KQ:
                        sp.wait_ge(s_zero[o % 2], (o + 1) // 2)
                    if o >= KQ:
                        sp.wait_ge(s_score, 2 * (o - KQ) + 2)
                    if o:
                        load_kq(sp, o, k_in[o % KQ], q_in[o % KQ], s_kq[o % KQ])

                def load_v(b):
                    if b >= 2:
                        sp.wait_ge(s_pv, NOCT * (b - 1))
                    sp.dma_start(v_place[b % 2][:], v_pad[b * P:(b + 1) * P, :]).then_inc(s_v[b % 2], 16)

                def store_x2(b):
                    sp.wait_ge(s_x2, 2 * b + 2)
                    sp.dma_start(x_mid[b * P:(b + 1) * P, :], x2[b % 2][:]).then_inc(s_x2st[b % 2], 16)

                def load_xb(b):
                    sp.dma_start(xb[b % 2][:], x_t[b * P:(b + 1) * P, :]).then_inc(s_xb[b % 2], 16)

                def load_dn(n):
                    if n >= 2:
                        sp.wait_ge(s_dlo, n - 1)
                    sp.dma_start(dn_raw[n % 2][:].rearrange("p (e r) -> p e r", e=NE),
                                 lora_down[:, n * P:(n + 1) * P, :].rearrange("e p r -> p e r")).then_inc(s_dn[n % 2], 16)

                def load_first(i):
                    sp.dma_start(first_y[i], x_mid[i * P:(i + 1) * P, :]).then_inc(s_first[i], 16)

                for o in range(OCTS):
                    b = o // NOCT
                    load_oct(o)
                    if o == 0:
                        sp.dma_start(bo_row[:], bo.partition_broadcast(P)).then_inc(s_bo, 16)
                    if DN_OCT <= o < DN_OCT + 2 * KC and o % 2 == 0:
                        load_dn((o - DN_OCT) // 2)
                    if o % NOCT == 1:
                        load_v(b)
                    if o % NOCT == NOCT - 1:
                        if b >= 2:
                            store_x2(b - 2)
                        load_xb(b)
                for i in range(2):
                    sp.wait_ge(s_x2st[i], 32)
                for i in (2, 3, 0, 1):
                    if i == 0:
                        sp.wait_ge(s_pv, NOCT * (NB - 1))
                    load_first(i)
                sp.wait_ge(s_pv, NOCT * NB)
                sp.dma_start(raw_d[0][0:NE, 0:NK], lora_keys).then_inc(s_raw_d[0], 16)
                sp.dma_start(raw_d[1], w_key).then_inc(s_raw_d[1], 16)
                store_x2(NB - 2)
                store_x2(NB - 1)
                for i in range(2):
                    sp.wait_ge(s_x2st[i], 16 * (NB // 2))

            @block.tensor
            def _(pe):
                for t in range(STEPS):
                    if t < QUADS:
                        o, slot = t // 2, t // 2 % KQ
                        if t % 2 == 0:
                            pe.wait_ge(s_kq[slot], 48 * (o // KQ + 1))
                        if t >= NSC:
                            pe.wait_ge(s_exp, t - NSC + 1)
                        for i in range(2):
                            p = 2 * (t % 2) + i
                            last = pe.matmul(sc_bank[t % NSC][:, i * 2 * P:(i + 1) * 2 * P], q_in[slot][:, p, :],
                                             k_in[slot][:, p, :, :].rearrange("r a k -> r (a k)"), start=True, stop=True)
                        last.then_inc(s_score, 1)
                    if T_LAG <= t < QUADS + T_LAG:
                        u = t - T_LAG
                        pe.wait_ge(s_norm, u + 1)
                        if u >= 2:
                            pe.wait_ge(s_ptc, u - 1)
                        for j in range(4):
                            last = pe.transpose(pt_bank[u % 2][:, j * P:(j + 1) * P], prob[u % NP][:, j, :], ident[:])
                        last.then_inc(s_pt, 1)
                    if oct_in_pv(t) is not None:
                        o = oct_in_pv(t)
                        b, h = o // NOCT, o // 4
                        pe.wait_ge(s_ptc, 2 * o + 2)
                        if o % NOCT == 0:
                            pe.wait_ge(s_v[b % 2], 16 * (b // 2 + 1))
                        if o % 4 == 0 and h >= 2:
                            pe.wait_ge(s_olo, h - 1)
                        for a in range(2):
                            for p in range(4):
                                last = pe.matmul(
                                    pv_bank[h % 2][32 * p:32 * p + 32, (o % 4) * P:(o % 4 + 1) * P],
                                    v_in[b % 2][:, 4 * (o % NOCT) + p, a, :], probT[o % 2][:, 2 * p + a, :],
                                    start=(a == 0), stop=(a == 1), skip_group_check=True)
                        last.then_inc(s_pv, 1)
                    if chunk_in_o(t):
                        b, half, k = chunk_in_o(t)
                        if k == 0:
                            pe.wait_ge(s_olo, 2 * b + 2)
                            if 0 < 2 * b + half < 2 * (NB - 1):
                                pe.wait_ge(s_x2, 2 * b + half)
                            if b == NB - 1:
                                pe.wait_ge(s_exp, QUADS)
                        cols = slice(half * HALF, (half + 1) * HALF)
                        hi, lo = oT_hi[b % 2], oT_lo[b % 2]
                        pe.matmul(out_bank(b, half)[:], hi[:, k, :], wo_hi[:, k, cols], start=(k == 0), stop=False)
                        pe.matmul(out_bank(b, half)[:], hi[:, k, :], wo_lo[:, k, cols], start=False, stop=False)
                        last = pe.matmul(out_bank(b, half)[:], lo[:, k, :], wo_hi[:, k, cols], start=False, stop=(k == KC - 1))
                        if k == KC - 1:
                            last.then_inc(s_o, 1)

            @block.scalar
            def _(act):
                for t in range(STEPS):
                    for n, (_, start, resume) in enumerate(NORMS):
                        if t == resume - 1:
                            norm.scalar_step(n)(act)
                    if t < QUADS:
                        act.wait_ge(s_max, t + 1)
                        if t >= NP:
                            act.wait_ge(s_pt, t - NP + 1)
                        for j in range(4):
                            last = act.activation(prob[t % NP][:, j, :], sc_bank[t % NSC][:, j * P:(j + 1) * P], ACT.Exp,
                                                  bias=negmax[:, t % NS, j:j + 1], accum_out=total[:, t % NS, j:j + 1])
                        last.then_inc(s_exp, 1)
                    if half_in_ev(t + 3) is not None:
                        h = half_in_ev(t + 3)
                        b = h // 2
                        act.wait_ge(s_pv, 4 * h + 4)
                        if b >= 2:
                            act.wait_ge(s_o, 2 * (b - 1))
                        act.activation(oT_hi[b % 2][:, 4 * (h % 2):4 * (h % 2) + 4, :].rearrange("p a b -> p (a b)"),
                                       pv_bank[h % 2][:], ACT.Copy).then_inc(s_ohi, 1)
                    if chunk_in_dn(t) is not None:
                        n = chunk_in_dn(t)
                        act.wait_ge(s_dn[n % 2], 16 * (n // 2 + 1))
                        act.activation(dn_hi[:, n, :], dn_raw[n % 2][:], ACT.Copy).then_inc(s_dhi, 1)

            @block.vector
            def _(dve):
                for i in range(2, KQ, 2):
                    dve.memset(k_in[i][:].bitcast(F32), 0.0).then_inc(s_zero[0], 1)
                for t in range(STEPS):
                    done = chunk_in_o(t - 1)
                    if done and done[2] == KC - 1:
                        b, half, _ = done
                        cols = slice(half * HALF, (half + 1) * HALF)
                        dve.wait_ge(s_o, 2 * b + half + 1)
                        dve.wait_ge(s_xbo, 2 * b + half + 1)
                        if half == 0 and b >= 2:
                            dve.wait_ge(s_x2st[b % 2], 16 * (b // 2))
                        dve.scalar_tensor_tensor(out=x2[b % 2][:, cols], in0=out_bank(b, half)[:], scalar=gates[:, 0:1],
                                                 in1=xb[b % 2][:, cols], op0=ALU.mult, op1=ALU.add).then_inc(s_x2, 1)
                    if t < QUADS:
                        dve.wait_ge(s_score, t + 1)
                        dve.tensor_reduce(negmax[:, t % NS, :], sc_bank[t % NSC][:].rearrange("p (j k) -> p j k", j=4),
                                          AX.X, ALU.max, negate=True).then_inc(s_max, 1)
                    if t == 2:
                        dve.wait_ge(s_bo, 16)
                        dve.tensor_scalar(bo_row[:], bo_row[:], gates[:, 0:1], None, ALU.mult).then_inc(s_bog, 1)
                    if 2 <= t < QUADS + 2:
                        n = (t - 2) % NS
                        dve.wait_ge(s_exp, t - 1)
                        dve.reciprocal(rec[:, n, :], total[:, n, :]).then_inc(s_rec, 1)
                    if T_LAG <= t < QUADS + T_LAG:
                        u = t - T_LAG
                        dve.wait_ge(s_pt, u + 1)
                        if u // 2 >= 2:
                            dve.wait_ge(s_pv, u // 2 - 1)
                        dve.tensor_copy(probT[u // 2 % 2][:, 4 * (u % 2):4 * (u % 2) + 4, :].rearrange("p a b -> p (a b)"),
                                        pt_bank[u % 2][:]).then_inc(s_ptc, 1)
                    if half_in_ev(t) is not None:
                        h = half_in_ev(t)
                        b, part = h // 2, slice(4 * (h % 2), 4 * (h % 2) + 4)
                        dve.wait_ge(s_ohi, h + 1)
                        dve.tensor_tensor(oT_lo[b % 2][:, part, :].rearrange("p a b -> p (a b)"), pv_bank[h % 2][:],
                                          oT_hi[b % 2][:, part, :].rearrange("p a b -> p (a b)").bitcast(F32),
                                          ALU.subtract).then_inc(s_olo, 1)
                    for n, (i, start, resume) in enumerate(NORMS):
                        if t in (start, start + 1, resume, resume + 1):
                            stages = norm.vector_stages(n, first_y[i], lambda dve: dve.wait_ge(s_first[i], 16))
                            stages[(start, start + 1, resume, resume + 1).index(t)](dve)

            @block.gpsimd
            def _(pool):
                for i in range(1, KQ, 2):
                    pool.memset(k_in[i][:].bitcast(F32), 0.0).then_inc(s_zero[1], 1)
                for t in range(QUADS + O_AT):
                    if t < QUADS:
                        pool.wait_ge(s_rec, t + 1)
                        pool.tensor_tensor(prob[t % NP][:], prob[t % NP][:],
                                           rec[:, t % NS, :].unsqueeze(2).to_broadcast([P, 4, P]), ALU.mult).then_inc(s_norm, 1)
                    b, step = (t - 18) // QB, (t - 18) % QB
                    if t >= 18 and b < NB and step in (0, 4):
                        half = step // 4
                        cols = slice(half * HALF, (half + 1) * HALF)
                        if half == 0:
                            pool.wait_ge(s_bog, 1)
                            pool.wait_ge(s_xb[b % 2], 16 * (b // 2 + 1))
                        pool.tensor_tensor(xb[b % 2][:, cols], xb[b % 2][:, cols], bo_row[:, cols], ALU.add).then_inc(s_xbo, 1)
                    n = chunk_in_dn(t - 1)
                    if n is not None:
                        pool.wait_ge(s_dhi, n + 1)
                        pool.tensor_tensor(dn_lo[:, n, :], dn_raw[n % 2][:], dn_hi[:, n, :].bitcast(F32),
                                           ALU.subtract).then_inc(s_dlo, 1)

        with ExitStack() as st, nc.Block() as block:
            wg_hi, wg_lo = place_a, place_c
            up_hi_tiles = arriving("up_hi_first", LC)
            up_hi = sb("up_hi", [P, LC, D], F32R, st)
            up_raw = arriving("up_raw", LC)
            up_lo = sb("up_lo", [P, LC, D], F32R, st)
            spare = arriving("spare_hi", 1, GB * D)
            yT_hi = sb("yT_hi", [P, GB + 1, KC, P], F32R, st)
            spare += arriving("spare_lo", 1, GB * D)
            yT_lo = sb("yT_lo", [P, GB + 1, KC, P], F32R, st)
            keysT = sb("keysT", [NK, NE], F32, st)
            key_w = sb("key_w", [P, KC, NE], F32, st)
            norm = LayerNorm("y", st)
            msum = sb("msum", [P, KC, GB], F32, st)
            score = sb("score", [GB, NE], F32, st)
            smax = sb("smax", [GB, 1], F32, st)
            expo = sb("expo", [GB, NE], F32, st)
            ssum = sb("ssum", [GB, 1], F32, st)
            coef = sb("coef", [GB, NE], F32, st)
            coefw = sb("coefw", [GB, NE, R], F32, st)
            coefc = sb("coefc", [P, LC, GB], F32, st)
            arrive = raw_d + spare + up_hi_tiles
            s_arrive = s_raw_d + [sem(f"s_arrive{i}") for i in range(2, len(arrive))]
            s_up = [sem(f"s_up{i}") for i in range(LC)]
            s_yin = [sem(f"s_yin{i}") for i in range(2)]
            s_xres = [sem(f"s_xres{i}") for i in range(2)]
            s_ost = [sem(f"s_ost{i}") for i in range(2)]
            s_small, s_smalle = sem("s_small"), sem("s_smalle")
            line, plan = new_line("d"), []
            ring = RawRing(line, plan, arrive, s_arrive, preloaded=2)
            t_end = {}
            ARRIVAL = [g * GB + i for g in range(NG) for i in ((0, 1, 2, 3) if g % 2 == 0 else (3, 0, 1, 2))]
            OUT_ORDER = [g * GB + i for g in range(NG) for i in ((1, 2, 3, 0) if g % 2 == 0 else (0, 1, 2, 3))]

            def slot_of(b):
                return b % GB + b // GB % 2

            def y_norm(n, job):
                b, slot, use = ARRIVAL[n], n % 2, (n - GB) // 2
                free = t_end[ARRIVAL[n - 2 if use else n - GB]]

                def load(sp):
                    line.wait_filled(sp, free)
                    sp.dma_start(yin[slot], x_mid[b * P:(b + 1) * P, :]).then_inc(s_yin[slot], 16)
                plan.append((free - 0.45, load))
                job.dve_pre = norm.vector_steps(n - GB, yin[slot], lambda dve: dve.wait_ge(s_yin[slot], 16 * (use + 1)))
                job.act_pre = norm.scalar_step(n - GB)

            def y_jobs(n):
                b = ARRIVAL[n]
                at = slot_of(b)
                tile, wait = (first_y[n], None) if n < GB else (yin[n % 2], norm.done(n - GB))
                t_end[b] = transpose_jobs(line, tile, wait, yT_hi[:, at, :, :], yT_lo[:, at, :, :],
                                          sums=msum[:, :, b % GB:b % GB + 1])

            def key_jobs():
                slot, landed = ring.take(lora_keys)
                end = line.add(Job(
                    lambda bank: nc.tensor.transpose(bank[:, 0:NE], arrive[slot][0:NE, 0:NK], ident[0:NE, 0:NE]),
                    lambda bank: nc.vector.tensor_copy(keysT[:], bank[:, 0:NE]), pe_wait=landed))
                ring.release(slot, end)
                slot2, landed2 = ring.take(w_key)

                def pe_fn(bank):
                    for k in range(KC):
                        last = nc.tensor.matmul(bank[:, k * NE:(k + 1) * NE], arrive[slot2][:, k * P:(k + 1) * P], keysT[:],
                                                start=True, stop=True)
                    return last
                end = line.add(Job(pe_fn, lambda bank: nc.vector.tensor_copy(key_w[:].rearrange("p k e -> p (k e)"),
                                                                             bank[:, 0:KC * NE]),
                                   pe_wait=landed2, reads=end))
                ring.release(slot2, end)
                return end

            def up_chunk(k):
                plan.append((-0.4, lambda sp: sp.dma_start(
                    up_raw[k],
                    lora_up.rearrange("e r o -> (e r) o")[k * P:(k + 1) * P, :]).then_inc(s_up[k], 16)))

                def landed(eng):
                    eng.wait_ge(s_up[k], 16)
                return line.add(Job(
                    None, lambda bank: nc.vector.tensor_tensor(up_lo[:, k, :], up_raw[k],
                                                               up_hi[:, k, :].bitcast(F32), ALU.subtract),
                    act=lambda bank: nc.scalar.activation(up_hi[:, k, :], up_raw[k], ACT.Copy),
                    act_wait=landed, dve_wait=landed))

            def score_job(g):
                def score_pe(bank):
                    for k in range(KC):
                        last = nc.tensor.matmul(bank[0:GB, 0:NE], msum[:, k, :], key_w[:, k, :],
                                                start=(k == 0), stop=(k == KC - 1))
                    return last

                def score_dve(bank):
                    link(nc.vector.tensor_reduce(smax[:], bank[0:GB, 0:NE], AX.X, ALU.max, negate=True))
                    link(nc.vector.tensor_scalar(score[:], bank[0:GB, 0:NE], smax[:, 0:1], None, ALU.add))
                    nc.vector.sem_inc(s_small, 1)
                    nc.vector.wait_ge(s_smalle, g + 1)
                    link(nc.vector.reciprocal(ssum[:], ssum[:]))
                    link(nc.vector.tensor_scalar(coef[:], expo[:], ssum[:, 0:1], None, ALU.mult))
                    return nc.vector.tensor_copy(coefw[:], coef[:].unsqueeze(2).to_broadcast([GB, NE, R]))

                def exponentials(act):
                    act.wait_ge(s_small, g + 1)
                    act.activation(expo[:], score[:], ACT.Exp, scale=1.0 / (S * NK ** 0.5),
                                   accum_out=ssum[:, 0:1]).then_inc(s_smalle, 1)
                return line.add(Job(score_pe, score_dve, reads=max(group_end(g), key_end), act_pre=exponentials))

            def spread_job(score_end):
                flat = coefw[:].rearrange("b e r -> b (e r)")

                def spread_pe(bank):
                    for c in range(LC):
                        last = nc.tensor.matmul(bank[:, c * GB:(c + 1) * GB], flat[:, c * P:(c + 1) * P],
                                                ident[0:GB, 0:GB], start=True, stop=True)
                    return last
                return line.add(Job(spread_pe, lambda bank: nc.vector.tensor_copy(coefc[:].rearrange("p c b -> p (c b)"),
                                                                                  bank[:, 0:LC * GB]), reads=score_end))

            def group_end(g):
                return max(t_end[b] for b in range(g * GB, (g + 1) * GB))

            def h_job(g, c, coef_end):
                def pe_fn(bank):
                    return three_products(
                        bank[:], lambda k: (dn_hi[:, k, c * P:(c + 1) * P], dn_lo[:, k, c * P:(c + 1) * P]),
                        lambda k: (yT_hi[:, g % 2:g % 2 + GB, k, :], yT_lo[:, g % 2:g % 2 + GB, k, :]), range(KC))

                def hi_fn(bank):
                    for i in range(GB):
                        tok = slice(i * P, (i + 1) * P)
                        last = nc.scalar.activation(h_hi[:, c, tok], bank[:, tok], ACT.Copy, scale=coefc[:, c, i:i + 1])
                    return last

                def lo_fn(bank):
                    for i in range(GB):
                        tok = slice(i * P, (i + 1) * P)
                        last = nc.vector.scalar_tensor_tensor(
                            out=h_lo[:, c, tok], in0=bank[:, tok], scalar=coefc[:, c, i:i + 1],
                            in1=h_hi[:, c, tok].bitcast(F32), op0=ALU.mult, op1=ALU.subtract)
                    return last
                return line.add(Job(pe_fn, lo_fn, act=hi_fn, reads=group_end(g),
                                    act_wait=lambda act: act.wait_ge(line.emptied, coef_end)))

            out_end = {}

            def out_job(n, half, h_end):
                b, slot = OUT_ORDER[n], n % 2
                i, at, cols = b % GB, slot_of(b), slice(half * HALF, (half + 1) * HALF)
                tok = slice(i * P, (i + 1) * P)

                def station(k):
                    if k == KC:
                        nc.tensor.wait_ge(line.emptied, h_end)
                    if k < KC:
                        return yT_hi[:, at, k, :], yT_lo[:, at, k, :]
                    return h_hi[:, k - KC, tok], h_lo[:, k - KC, tok]

                def moving(k):
                    if k < KC:
                        return wg_hi[:, k, cols], wg_lo[:, k, cols]
                    return up_hi[:, k - KC, cols], up_lo[:, k - KC, cols]
                part = raw_d[slot][:, cols]
                job = Job(
                    lambda bank: three_products(bank[:], station, moving, range(KC + LC)),
                    lambda bank: nc.vector.scalar_tensor_tensor(
                        out=part, in0=bank[:], scalar=gates[:, 1:2], in1=part, op0=ALU.mult, op1=ALU.add),
                    reads=base_end, dve_wait=lambda dve: dve.wait_ge(s_xres[slot], 16 * (n // 2 + 1)))
                end = line.add(job)
                if half == 0:
                    def load(sp):
                        if n < 2:
                            sp.wait_ge(line.emptied, base_end)
                        else:
                            sp.wait_ge(s_ost[slot], 16 * (n // 2))
                        sp.dma_start(raw_d[slot], x_mid[b * P:(b + 1) * P, :]).then_inc(s_xres[slot], 16)
                    plan.append((base_end + 0.1 if n < 2 else out_end[n - 2] + 0.8, load))
                else:
                    def store(sp):
                        sp.wait_ge(line.emptied, end)
                        sp.dma_start(out_t[b * P:(b + 1) * P, :], raw_d[slot]).then_inc(s_ost[slot], 16)
                    out_end[n] = end
                    plan.append((end + 0.6, store))
                return job

            def base_chunks(n):
                nonlocal chunk
                for _ in range(n):
                    end, _ = weight_chunk(line, ring, w_org, chunk, wg_hi, wg_lo)
                    chunk += 1
                return end

            chunk = 0
            key_end = key_jobs()
            for n in range(GB):
                y_jobs(n)
            score_end = score_job(0)
            base_chunks(1)
            coef_end = spread_job(score_end)
            for g in range(NG):
                for c in range(LC):
                    h_end = h_job(g, c, coef_end)
                    carrier = line.jobs[-1]
                    if g == 0:
                        base_end = base_chunks(1 if c == 0 else 2)
                if g == 0:
                    for k in range(LC):
                        h_end = up_chunk(k)
                for i in range(GB):
                    n, more = g * GB + i, g + 1 < NG
                    if more:
                        y_norm(n + GB, carrier)
                        y_jobs(n + GB)
                    carrier = out_job(n, 0, h_end)
                    if more and i == GB - 1:
                        score_end = score_job(g + 1)
                    out_job(n, 1, h_end)
                    if more and i == GB - 1:
                        coef_end = spread_job(score_end)

            def stores_end(sp):
                for i in range(2):
                    sp.wait_ge(s_ost[i], 16 * (NB // 2))
            run_phase(block, line, plan, stores_end)


_INS = ['x', 'ctx_4096', 'g_xattn', 'g_ffn', 'L0_xattn_Wq', 'L0_xattn_bq', 'L0_xattn_Wk', 'L0_xattn_bk',
        'L0_xattn_Wv', 'L0_xattn_bv', 'L0_xattn_interference', 'L0_xattn_amp', 'L0_xattn_Wo', 'L0_xattn_bo',
        'L0_ffn_W_org', 'L0_ffn_lora_down', 'L0_ffn_lora_up', 'L0_ffn_lora_keys', 'L0_ffn_Wq']


def kernel(**inputs):
    import numpy as np
    import concourse.bacc as bacc
    from concourse.bass_utils import run_bass_kernel_spmd

    nc = bacc.Bacc("TRN2", target_bir_lowering=False, num_devices=1)
    arrays, args = {}, []
    for name in _INS:
        a = np.ascontiguousarray(inputs[name])
        arrays[f"in_{name}"] = a
        args.append(nc.dram_tensor(f"in_{name}", a.shape, mybir.dt.from_np(a.dtype), kind="ExternalInput").ap())
    args.append(nc.dram_tensor("out_x", inputs['x'].shape, F32, kind="ExternalOutput").ap())
    build(nc, *args)
    r = run_bass_kernel_spmd(nc, [arrays], core_ids=[0])
    return r.results[0]["out_x"]
```
